# Optimizing a Trainium2 kernel written in Bass

```python
import numpy as np
import jax
import jax.numpy as jnp

def _softmax(x, axis=-1):
    return jax.nn.softmax(x, axis=axis)

def _gelu(x):
    return jax.nn.gelu(x, approximate=True)

def _silu(x):
    return jax.nn.silu(x)

def _sigmoid(x):
    return jax.nn.sigmoid(x)

def _layernorm(x, axis=-1, eps=1e-05):
    m = jnp.mean(x, axis=axis, keepdims=True)
    v = jnp.var(x, axis=axis, keepdims=True)
    return (x - m) / jnp.sqrt(v + eps)

def _scatter_add(tgt, idx, src, axis=0):
    return tgt.at[idx].add(src)

def _segment_sum(src, seg, n):
    return jax.ops.segment_sum(src, seg, n)
kernel_name = 'mk_gnn_preln_d2_gnn_r32_3b72fb'

def setup_inputs(seed: int=0):
    np.random.seed(seed)
    _w = jnp.asarray

    def _rec_inputs():
        import jax
        import jax.numpy as jnp
        _gk = jax.random.key(seed)
        x = -0.000929 + 1 * jax.random.normal(jax.random.fold_in(_gk, 1), (3125, 32), jnp.float32)
        _s = jax.random.randint(jax.random.fold_in(_gk, 2), (50000,), 0, 3125, jnp.int32)
        _d = jax.random.randint(jax.random.fold_in(_gk, 3), (50000,), 0, 3125, jnp.int32)
        _loop = jnp.arange(3125, dtype=jnp.int32)
        src = jnp.concatenate([_s, _d, _loop])
        dst = jnp.concatenate([_d, _s, _loop])
        _o = jnp.argsort(dst, stable=True)
        src = src[_o]
        dst = dst[_o]
        edge_attr_4 = 0.00086875 + 0.999764 * jax.random.normal(jax.random.fold_in(_gk, 12), (103125, 4), jnp.float32)
        edge_attr_8 = jax.random.uniform(jax.random.fold_in(_gk, 13), (103125, 8), jnp.float32, 0.0, 1)
        return (x, src, dst, edge_attr_4, edge_attr_8)
    x, src, dst, edge_attr_4, edge_attr_8 = _rec_inputs()

    def _L0_gnn_setup():
        import jax, jax.numpy as jnp
        import numpy as np
        N = 1024
        E = 16384
        MUL = 8
        NB = 8
        HR = 64
        NTP = 4 * MUL * MUL
        AVG_NEI = 16.0
        INV_SQRT3 = 1.0 / np.sqrt(3.0)
        ALPHA = 1.0 / np.sqrt(2.0 * MUL)
        key = jax.random.key(seed)
        ks = jax.random.split(key, 12)
        h = jax.random.normal(ks[0], (N, 4 * MUL), jnp.float32)
        edge_index = jax.random.randint(ks[1], (2, E), 0, N)
        edge_sh = jax.random.normal(ks[2], (E, 4), jnp.float32)
        edge_radial = jax.random.uniform(ks[3], (E, NB), jnp.float32)

        def lin(k, fi, fo):
            return (jax.random.normal(k, (fi, fo), jnp.float32) / np.sqrt(fi)).astype(jnp.float32)
        W1 = lin(ks[4], NB, HR)
        b1 = jnp.zeros((HR,), jnp.float32)
        W2 = lin(ks[5], HR, HR)
        b2 = jnp.zeros((HR,), jnp.float32)
        W3 = lin(ks[6], HR, NTP)
        b3 = jnp.zeros((NTP,), jnp.float32)
        Ws = jax.random.normal(ks[7], (MUL, MUL), jnp.float32)
        Wv = jax.random.normal(ks[8], (MUL, MUL), jnp.float32)
        return dict(h=h, edge_index=edge_index, edge_sh=edge_sh, edge_radial=edge_radial, n_atoms=N, W1=W1, b1=b1, W2=W2, b2=b2, W3=W3, b3=b3, Ws=Ws, Wv=Wv)
    _L0_gnn_all = _L0_gnn_setup()
    _L0_gnn_in = {k: v for k, v in _L0_gnn_all.items() if k in ('W1', 'b1', 'W2', 'b2', 'W3', 'b3', 'Ws', 'Wv')}
    del _L0_gnn_all

    def _L1_gnn_setup():
        import jax, jax.numpy as jnp
        import numpy as np
        N_NODES = 3125
        N_EDGES = 50000
        D_FEAT = 32
        key = jax.random.key(seed)
        k1, k2, k3 = jax.random.split(key, 3)
        h = jax.random.normal(k1, (N_NODES, D_FEAT), dtype=jnp.float32)
        src = jax.random.randint(k2, (N_EDGES,), 0, N_NODES, dtype=jnp.int64)
        dst = jax.random.randint(k3, (N_EDGES,), 0, N_NODES, dtype=jnp.int64)
        return {'h': h, 'src': src, 'dst': dst}
    _L1_gnn_all = _L1_gnn_setup()
    _L1_gnn_in = {k: v for k, v in _L1_gnn_all.items() if k in ()}
    del _L1_gnn_all
    return {'x': x, 'src': src, 'dst': dst, 'edge_attr_4': edge_attr_4, 'edge_attr_8': edge_attr_8, 'L0_gnn_W1': _L0_gnn_in['W1'], 'L0_gnn_b1': _L0_gnn_in['b1'], 'L0_gnn_W2': _L0_gnn_in['W2'], 'L0_gnn_b2': _L0_gnn_in['b2'], 'L0_gnn_W3': _L0_gnn_in['W3'], 'L0_gnn_b3': _L0_gnn_in['b3'], 'L0_gnn_Ws': _L0_gnn_in['Ws'], 'L0_gnn_Wv': _L0_gnn_in['Wv']}

def reference(x, src, dst, edge_attr_4, edge_attr_8, L0_gnn_W1, L0_gnn_b1, L0_gnn_W2, L0_gnn_b2, L0_gnn_W3, L0_gnn_b3, L0_gnn_Ws, L0_gnn_Wv):
    import jax
    import jax.numpy as jnp

    def _L0_gnn_ref(h, edge_index, edge_sh, edge_radial, n_atoms, W1, b1, W2, b2, W3, b3, Ws, Wv):
        import jax, jax.numpy as jnp
        import numpy as np
        N = 1024
        E = 16384
        MUL = 8
        NB = 8
        HR = 64
        NTP = 4 * MUL * MUL
        AVG_NEI = 16.0
        INV_SQRT3 = 1.0 / np.sqrt(3.0)
        ALPHA = 1.0 / np.sqrt(2.0 * MUL)
        src, dst = (edge_index[0], edge_index[1])
        x = jax.nn.silu(edge_radial @ W1 + b1)
        x = jax.nn.silu(x @ W2 + b2)
        tpw = x @ W3 + b3
        P = MUL * MUL
        W00 = tpw[:, 0 * P:1 * P].reshape(-1, MUL, MUL)
        W110 = tpw[:, 1 * P:2 * P].reshape(-1, MUL, MUL)
        W01 = tpw[:, 2 * P:3 * P].reshape(-1, MUL, MUL)
        W10 = tpw[:, 3 * P:4 * P].reshape(-1, MUL, MUL)
        hs = h[:, :MUL]
        hv = h[:, MUL:].reshape(-1, MUL, 3)
        hs_e = hs[src]
        hv_e = hv[src]
        sh0 = edge_sh[:, 0]
        sh1 = edge_sh[:, 1:4]
        m0 = ALPHA * (jnp.einsum('eu,euw->ew', hs_e * sh0[:, None], W00) + INV_SQRT3 * jnp.einsum('eui,ei,euw->ew', hv_e, sh1, W110))
        m1 = ALPHA * (jnp.einsum('eu,ei,euw->ewi', hs_e, sh1, W01) + jnp.einsum('eui,euw->ewi', hv_e * sh0[:, None, None], W10))
        messages = jnp.concatenate([m0, m1.reshape(-1, 3 * MUL)], axis=-1)
        agg = jax.ops.segment_sum(messages, dst, num_segments=n_atoms) / np.sqrt(AVG_NEI)
        self0 = hs @ Ws / np.sqrt(MUL)
        self1 = jnp.einsum('nui,uw->nwi', hv, Wv) / np.sqrt(MUL)
        h_self = jnp.concatenate([self0, self1.reshape(-1, 3 * MUL)], axis=-1)
        return h_self + agg

    def _L1_gnn_ref(h, src, dst):
        import jax, jax.numpy as jnp
        import numpy as np
        N_NODES = 3125
        N_EDGES = 50000
        D_FEAT = 32
        n = h.shape[0]
        msg_sum = jax.ops.segment_sum(h[src], dst, num_segments=n)
        deg = jax.ops.segment_sum(jnp.ones_like(dst, dtype=h.dtype), dst, num_segments=n)
        h_N = msg_sum / jnp.maximum(deg, 1.0)[:, None]
        return h_N
    edge_index = jnp.stack([src, dst])
    h = jnp.maximum(_layernorm(x, axis=-1), 0.0)
    x = x + _L0_gnn_ref(h, edge_index, edge_attr_4, edge_attr_8, 3125, L0_gnn_W1, L0_gnn_b1, L0_gnn_W2, L0_gnn_b2, L0_gnn_W3, L0_gnn_b3, L0_gnn_Ws, L0_gnn_Wv)
    h = jnp.maximum(_layernorm(x, axis=-1), 0.0)
    x = x + _L1_gnn_ref(h, src, dst)
    return x

_drawn_inputs = setup_inputs


def setup_inputs(seed=0):
    import zlib

    import numpy as np

    out = dict(_drawn_inputs(seed))
    spreads = {'L0_gnn_b1': (0.0, 0.366), 'L0_gnn_b2': (0.0, 0.1), 'L0_gnn_b3': (0.0, 0.1)}
    factors = {}
    for name, (base, spread) in spreads.items():
        noise = np.random.default_rng([zlib.crc32(name.encode()), seed]).standard_normal(out[name].shape)
        drawn = base * np.exp(spread * noise) if base else spread * noise
        out[name] = jnp.asarray(drawn.astype(out[name].dtype))
    for name, factor in factors.items():
        out[name] = (out[name] * factor).astype(out[name].dtype)
    return out
```

```python
from contextlib import ExitStack

import concourse.bass as bass
from concourse import mybir

F32 = mybir.dt.float32
BF16 = mybir.dt.bfloat16
FP16 = mybir.dt.float16
I32 = mybir.dt.int32
ALU = mybir.AluOpType
ACT = mybir.ActivationFunctionType
X = mybir.AxisListType.X

P = 128
N, F, E = 3125, 32, 103125
MUL, HR, NB = 8, 64, 8
NTP = 4 * MUL * MUL
TG = 8
TH = TG // 2
GROUPS = -(-E // (TG * P))
TILES = GROUPS * TG
BLOCKS = -(-N // P)
LAST = N - (BLOCKS - 1) * P
WT = 8
WG = 64
US = MUL + 1
VEC = 3 * US * MUL
MV = VEC + MUL
KEYS = BLOCKS * WT
COLS = BLOCKS * P
ACOLS = 3136
NF = BLOCKS * F
SPAN = 16
BANKS, BANK = 7, ACOLS // 7
PARTS = 2 * F + 1
BB = 7
HALVES = ((0, 9), (9, BLOCKS))
LOW = 2048.0
POOL_ROWS, ACT_ROWS = 11, 2
EARLY = 19
EPS = 1e-5
C_MSG = (2.0 * MUL) ** -0.5 / 16.0 ** 0.5
C_VEC = C_MSG / 3.0 ** 0.5
C_SELF = MUL ** -0.5


def build(nc, x, src, dst, first, sh, rad, w1, w2, w3, bias12, b3, wself, perm, ident, spread, out):
    h_table = nc.dram_tensor("h_table", (COLS, F), F32, kind="Internal").ap()
    msg_table = nc.dram_tensor("msg_table", (GROUPS, P, TG * F), F32, kind="Internal").ap()
    ctx = ExitStack()
    with ctx:
        def sb(name, shape, dt):
            return ctx.enter_context(nc.sbuf_tensor(name, shape, dt))

        def sem(name):
            return ctx.enter_context(nc.semaphore(name))

        ps = ctx.enter_context(nc.psum_tensor("ps", [P, 8, 512], F32))
        mlp_ps = ps[:, 0, :]
        tpw_ps = ps[:, 1:5, :].rearrange("p (h b) n -> p h (b n)", h=2)
        cnt_ps = ps[:, 5:7, 0:2 * KEYS]
        agg_ps = ps[0:WG, 7, 0:MV]
        turn_ps = ps[0:F, 7, 256:256 + WG]

        counts = sb("counts", [P, BLOCKS, ACOLS], FP16)
        packed = sb("packed", [P, COLS], F32)
        agg_t = packed[0:F, :]
        rad_sb = packed[32:32 + 2 * NB, 0:2048].rearrange("p (s n) -> p s n", s=4)
        w1_sb = packed[32:32 + 2 * NB, 2048:2048 + P]
        first_sb = packed[64:65, 0:TILES].bitcast(I32)
        tables = sb("tables", [P, 3, TILES], FP16)
        stat = sb("stat", [P, 4, BLOCKS], F32)
        zero = sb("zero", [P, 1], F32)
        checks = sb("checks", [P, 8], F32)
        dense_sb = sb("dense_sb", [1, 1], I32)
        w2_sb = sb("w2_sb", [P, P], F32)
        w3_sb = sb("w3_sb", [P, NTP], F32)
        b12_sb = sb("b12_sb", [P, 2], F32)
        b3_rows = sb("b3_rows", [P, NTP], BF16)
        ones_bf = sb("ones_bf", [P, P], BF16)
        wself_sb = sb("wself_sb", [F, F], F32)
        perm_sb = sb("perm_sb", [F, F], F32)
        iota_a = sb("iota_a", [P, P], FP16)
        iota_k = sb("iota_k", [P, KEYS], FP16)
        iota_w = sb("iota_w", [P, WG], F32)

        sh_sb = sb("sh_sb", [P, 4, TG, 4], F32)
        idx_sb = sb("idx_sb", [P, 4, TG], I32)
        h_src = sb("h_src", [P, 4, TG, F], F32)
        y2 = sb("y2", [P, 2, 512], F32)
        lhs = sb("lhs", [P, 2, TG, 2 * MUL + F], F32)
        lhs_v = lhs[:, :, :, 3 * MUL:].rearrange("p s t (u i) -> p s t i u", i=3)
        hv_sh1 = sb("hv_sh1", [P, TG, MUL, 3], F32)
        cur = sb("cur", [P, 4, 3, TG], F32)
        hot = sb("hot", [P, TH * P + TH * KEYS + TG * WG], F32)
        oh_a = hot[:, 0:TH * P].bitcast(FP16).rearrange("p (s t n) -> p s t n", s=2, t=TH)
        oh_k = hot[:, TH * P:TH * (P + KEYS)].bitcast(FP16).rearrange("p (s t n) -> p s t n", s=2, t=TH)
        oh_w = hot[:, TH * (P + KEYS):].rearrange("p (t n) -> p t n", t=TG)
        work = sb("work", [P, TH * 192 + TG * MV], F32)
        prod_s = work[:, 0:TH * 192].rearrange("p (t n) -> p t n", t=TH)
        terms = work[:, TH * 192:].rearrange("p (t n) -> p t n", t=TG)
        vec_terms = terms[:, :, 0:VEC].rearrange("p t (i n) -> p t i n", i=3)
        t01 = sb("t01", [P, TH, MUL], F32)
        agg_sb = sb("agg_sb", [WG, F], F32)
        ident_w = sb("ident_w", [WG, WG], F32)
        stage = sb("stage", [P, 2, 2, KEYS], FP16)

        early = counts[:, EARLY:BLOCKS, :].rearrange("p a b -> p (a b)").bitcast(F32)

        def carve(flat, start, n):
            return flat[:, start:start + n]

        def cleared(first_row, end):
            return counts[:, first_row:end, :].rearrange("p a b -> p (a b)").bitcast(F32)

        def nodes(flat):
            return flat.rearrange("p (b f) -> p b f", f=F)

        src_all, dst_all, first_bc, scratch_i = (carve(early, k * TILES, TILES).bitcast(I32) for k in range(4))
        scratch_f = carve(early, 4 * TILES, TILES)
        x_in, h_in, xc_in, sq_in = (nodes(carve(early, 5 * TILES + k * NF, NF)) for k in range(4))
        free = counts[:, 0:EARLY, :].rearrange("p a b -> p (a b)").bitcast(F32)
        iota_all = free[:, 0:ACOLS]
        oh_all = free[:, ACOLS:3 * ACOLS].rearrange("p (s n) -> p s n", s=2)
        rows = free[:, 3 * ACOLS:3 * ACOLS + 4 * TG * (F + 1)].rearrange("p (s t f) -> p s t f", s=4, t=TG)
        msg = free[:, 4 * ACOLS - TG * F:4 * ACOLS].rearrange("p (t f) -> p t f", t=TG)
        sums_t = free[0:F + 1, 4 * ACOLS:5 * ACOLS]
        spread_sb = free[0:F + 1, 5 * ACOLS:5 * ACOLS + PARTS]
        x_turned = nodes(carve(early, 5 * TILES + 4 * NF + P + 2 * NTP + 3 * NTP // 2, NF))
        ident_sb = carve(early, 5 * TILES + 4 * NF, P)
        b3_f = carve(early, 5 * TILES + 4 * NF + P, 2 * NTP)[0:1, :].rearrange("p (a n) -> p a n", a=2)
        b3_parts = carve(early, 5 * TILES + 4 * NF + P + 2 * NTP, 3 * NTP // 2)[0:1, :].bitcast(BF16).rearrange("p (a n) -> p a n", a=3)
        x_1, h_1, xc_1 = (nodes(carve(work[:, :], k * NF, NF)) for k in range(3))
        sq_1 = nodes(y2[:, :, :].rearrange("p a b -> p (a b)")[:, 0:NF])
        parts = hot.bitcast(FP16)[:, 0:BLOCKS * PARTS].rearrange("p (b f) -> p b f", f=PARTS)

        s_in = sem("s_in")
        s_mlp = sem("s_mlp")
        s_x = sem("s_x")
        s_zero = sem("s_zero")
        s_turned = sem("s_turned")
        s_root = sem("s_root")
        s_edges = sem("s_edges")
        s_init = sem("s_init")
        s_iota = sem("s_iota")
        s_b3 = sem("s_b3")
        s_b3rows = sem("s_b3rows")
        s_htab = sem("s_htab")
        s_ht = sem("s_ht")
        s_htc = sem("s_htc")
        s_self = sem("s_self")
        s_selfc = sem("s_selfc")
        s_rad = [sem(f"s_rad{k}") for k in range(4)]
        s_sh = [sem(f"s_sh{k}") for k in range(4)]
        s_gather = [sem(f"s_gather{k}") for k in range(4)]
        s_idx = [sem(f"s_idx{k}") for k in range(4)]
        s_product = sem("s_product")
        s_dot = sem("s_dot")
        s_prep = sem("s_prep")
        s_copied = sem("s_copied")
        s_l1, s_y1, s_l2, s_y2 = sem("s_l1"), sem("s_y1"), sem("s_l2"), sem("s_y2")
        s_tpw, s_prod, s_sum, s_msg, s_whole = sem("s_tpw"), sem("s_prod"), sem("s_sum"), sem("s_msg"), sem("s_whole")
        s_cur, s_dist, s_far, s_lane, s_key, s_place = sem("s_cur"), sem("s_dist"), sem("s_far"), sem("s_lane"), sem("s_key"), sem("s_place")
        s_addc = sem("s_addc")
        s_t01 = sem("s_t01")
        s_cnt, s_stage = sem("s_cnt"), sem("s_stage")
        s_agg, s_aggred, s_turn, s_aggadd = sem("s_agg"), sem("s_aggred"), sem("s_turn"), sem("s_aggadd")
        s_turning = sem("s_turning")
        s_x1, s_x1c, s_fin, s_parts, s_mean, s_res, s_out = (sem("s_x1"), sem("s_x1c"), sem("s_fin"), sem("s_parts"), sem("s_mean"),
                                                      sem("s_res"), sem("s_out"))
        s_check, s_verdict, s_dense = sem("s_check"), sem("s_verdict"), sem("s_dense")
        s_stored = sem("s_stored")
        s_ready, s_all, s_scat, s_scats, s_sumst, s_spread = (sem("s_ready"), sem("s_all"), sem("s_scat"), sem("s_scats"),
                                                              sem("s_sumst"), sem("s_spread"))
        s_rows = [sem(f"s_rows{k}") for k in range(4)]
        s_grows = [sem(f"s_grows{k}") for k in range(4)]
        s_layer0, s_cleared, s_alliota = sem("s_layer0"), sem("s_cleared"), sem("s_alliota")
        s_h1 = sem("s_h1")
        s_fetch, s_go = sem("s_fetch"), sem("s_go")
        block = ctx.enter_context(nc.Block())

        def result_ps(b):
            return ps[:, b // BB, (b % BB) * PARTS:(b % BB + 1) * PARTS]

        S_VAR = 7
        S_H = 13
        S_HALF = 14

        def every_group(eng, step):
            step(0, 0, 1, True, False)
            rounds = (GROUPS - 2) // 4
            with eng.Fori(0, rounds) as i:
                for k in range(1, 5):
                    step(4 * i + k, k % 4, i + 1 + k // 4, False, False)
            for g in range(4 * rounds + 1, GROUPS):
                step(g, g % 4, g // 4 + 1, False, g == GROUPS - 1)

        def dense(eng):
            eng.wait_ge(s_dense, 1)
            return nc.values_load(dense_sb[0:1, 0:1], engines=[eng.engine], min_val=0, max_val=1,
                                  skip_runtime_bounds_check_because="a comparison's result")

        def general(eng):
            return 1 - dense(eng)

        def fetch_groups(eng, step):
            for k in range(4):
                step(k, k, 1, True, False)
            rounds = (GROUPS - 5) // 4
            with eng.Fori(0, rounds) as i:
                for k in range(4):
                    step(4 * i + 4 + k, k, i + 2, False, False)
            for g in range(4 * rounds + 4, GROUPS):
                step(g, g % 4, g // 4 + 1, False, g == GROUPS - 1)

        @block.sync
        def _(sp):
            full = BLOCKS - 1
            def load(g, slot, wait):
                if wait:
                    sp.wait_ge(s_l1, g - 3)
                    sp.wait_ge(s_prep, g - 3)
                    sp.wait_ge(s_msg, 2 * g - 6)
                sp.dma_start(rad_sb[:, slot, :], rad[bass.ds(g, 1), :, :].rearrange("a p n -> (a p) n")).then_inc(s_rad[slot], 16)
                sp.dma_start(idx_sb[:, slot, :], src[:, bass.ds(g * TG, TG)]).then_inc(s_idx[slot], 16)
                sp.dma_start(sh_sb[:, slot, :, :], sh[bass.ds(g, 1), :, :].rearrange("a p (t c) -> (a p) t c", c=4)).then_inc(s_sh[slot], 16)

            sp.wait_ge(s_init, 1)
            sp.dma_start(x_in[:, 0:full, :], x[0:full * P, :].rearrange("(b p) f -> p b f", p=P)).then_inc(s_x, 16)
            sp.dma_start(x_in[0:LAST, full, :], x[full * P:N, :]).then_inc(s_x, 16)
            for to, fr in ((w1_sb, w1), (b12_sb[:, :], bias12), (w2_sb[:, :], w2)):
                sp.dma_start(to, fr).then_inc(s_mlp, 16)
            load(0, 0, False)
            for to, fr in ((ident_sb, ident), (w3_sb[:, :], w3), (wself_sb[:, :], wself), (perm_sb[:, :], perm),
                           (ident_w[:, :], ident[0:WG, 0:WG])):
                sp.dma_start(to, fr).then_inc(s_in, 16)
            sp.dma_start(b3_f[:, 0, :], b3).then_inc(s_in, 16)
            sp.dma_start(first_sb, first).then_inc(s_in, 16)
            sp.dma_start(src_all, src).then_inc(s_edges, 16)
            sp.dma_start(dst_all, dst).then_inc(s_edges, 16)
            sp.dma_start(first_bc, first.partition_broadcast(P)).then_inc(s_edges, 16)
            load(1, 1, False)
            sp.wait_ge(s_init, S_H)
            sp.dma_start(h_table.rearrange("(b p) f -> p b f", p=P), h_in).then_inc(s_htab, 16)
            load(2, 2, False)
            load(3, 3, False)
            sp.wait_ge(s_b3, 4)
            for half in range(2):
                for j in range(3):
                    sp.dma_start(b3_rows[64 * half + j:64 * half + j + 1, :], b3_parts[:, j, :]).then_inc(s_b3rows, 16)

            def loads(g, slot, use, first_step, last):
                load(g + 4, slot, True)
            loads(0, 0, 1, True, False)
            rounds = (GROUPS - 6) // 4
            with sp.Fori(0, rounds) as i:
                for k in range(1, 5):
                    loads(4 * i + k, k % 4, i + 1, False, False)
            for g in range(4 * rounds + 1, GROUPS - 4):
                loads(g, g % 4, 1, False, True)
            with sp.If(general(sp)):
                sp.wait_ge(s_stored, 16 * GROUPS)
                sp.wait_ge(s_ready, 1)

                def fetch(g, slot, use, first_step, last):
                    if not first_step:
                        sp.wait_ge(s_scats, TG * g - 3 * TG)
                    sp.dma_start(rows[:, slot, :, 0:F], msg_table[bass.ds(g, 1), :, :].rearrange("a p (t f) -> (a p) t f", f=F)).then_inc(s_rows[slot], 16)
                fetch_groups(sp, fetch)
            with sp.If(general(sp)):
                sp.dma_start(spread_sb, spread).then_inc(s_spread, 16)
                sp.wait_ge(s_h1, 2)
                sp.dma_start(h_table.rearrange("(b p) f -> p b f", p=P), h_1).then_inc(s_htab, 16)
            for k, b in enumerate(range(0, full, BB)):
                sp.wait_ge(s_res, k + 1)
                n = min(BB, full - b)
                sp.dma_start(out[b * P:(b + n) * P, :].rearrange("(b p) f -> p b f", p=P), h_1[:, b:b + n, :]).then_inc(s_out, 16)
            sp.dma_start(out[full * P:N, :], h_1[0:LAST, full, :]).then_inc(s_out, 16)
            sp.wait_ge(s_out, 16 * (-(-full // BB) + 1))
            sp.wait_ge(s_htab, 16)

        @block.gpsimd
        def _(pool):
            nc.gpsimd.iota(iota_a[:, :], pattern=[[1, P]], base=0, channel_multiplier=0, allow_small_or_imprecise_dtypes=True).then_inc(s_iota, 1)
            nc.gpsimd.iota(iota_k[:, :], pattern=[[1, KEYS]], base=0, channel_multiplier=0, allow_small_or_imprecise_dtypes=True).then_inc(s_iota, 1)
            nc.gpsimd.iota(iota_w[:, :], pattern=[[1, WG]], base=0, channel_multiplier=0, allow_small_or_imprecise_dtypes=True).then_inc(s_iota, 1)
            nc.gpsimd.memset(cleared(0, POOL_ROWS), 0.0).then_inc(s_cleared, 1)
            pool.wait_ge(s_htab, 16)

            def gather(slot, use):
                pool.wait_ge(s_idx[slot], 16 * use)
                pool.sem_inc(s_go, 1)
                for t in range(TG):
                    nc.gpsimd.indirect_dma_start(
                        h_src[:, slot, t, :], None, h_table,
                        bass.IndirectOffsetOnAxis(ap=idx_sb[:, slot, t:t + 1], axis=0)).then_inc(s_gather[slot], 16)

            def prepare(g, slot, use, first_step, last):
                if not last:
                    if not first_step:
                        pool.wait_ge(s_product, g)
                        pool.wait_ge(s_copied, g)
                    gather((slot + 1) % 4, use + (slot == 3))
                pool.wait_ge(s_gather[slot], 16 * TG * use)
                pool.wait_ge(s_sh[slot], 16 * use)
                if not first_step:
                    pool.wait_ge(s_prod, 2 * g - 1)
                    pool.wait_ge(s_dot, g)
                hv = h_src[:, slot, :, MUL:F].rearrange("p t (u i) -> p t u i", i=3)
                nc.gpsimd.tensor_tensor(hv_sh1[:, :, :, :], hv, sh_sb[:, slot, :, 1:4].unsqueeze(2).to_broadcast((P, TG, MUL, 3)),
                                        ALU.mult).then_inc(s_product, 1)
                nc.gpsimd.tensor_tensor(lhs[:, slot % 2, :, 2 * MUL:], h_src[:, slot, :, :],
                                        sh_sb[:, slot, :, 0:1].to_broadcast((P, TG, F)), ALU.mult).then_inc(s_prep, 1)

            gather(0, 1)
            every_group(pool, prepare)
            with pool.If(general(pool)):
                pool.wait_ge(s_cleared, 3)
                nc.gpsimd.iota(iota_all, pattern=[[1, ACOLS]], base=0, channel_multiplier=0,
                               allow_small_or_imprecise_dtypes=True).then_inc(s_alliota, 1)
                pool.wait_ge(s_htab, 32)
                pool.wait_ge(s_scats, TILES)

                def regather(g, slot, use, first_step, last):
                    if not first_step:
                        pool.wait_ge(s_scats, TILES + TG * g - 3 * TG)
                    nc.gpsimd.tensor_copy(idx_sb[:, slot, :], src_all[:, bass.ds(g * TG, TG)]).then_inc(s_fetch, 1)
                    pool.wait_ge(s_fetch, g + 1)
                    pool.sem_inc(s_go, 1)
                    for t in range(TG):
                        nc.gpsimd.indirect_dma_start(
                            rows[:, slot, t, 0:F], None, h_table,
                            bass.IndirectOffsetOnAxis(ap=idx_sb[:, slot, t:t + 1], axis=0)).then_inc(s_grows[slot], 16)
                fetch_groups(pool, regather)

        @block.tensor
        def _(pe):
            def layer1(g, slot, use):
                pe.wait_ge(s_rad[slot], 16 * use)
                if not (isinstance(g, int) and g == 0):
                    pe.wait_ge(s_y2, 2 * g)
                nc.tensor.matmul(mlp_ps, w1_sb, rad_sb[:, slot, :], start=True, stop=True).then_inc(s_l1, 1)

            def layer2(g, slot):
                pe.wait_ge(s_y1, g + 1)
                nc.tensor.matmul(mlp_ps, w2_sb[:, :], y2[:, slot % 2, :], start=True, stop=True).then_inc(s_l2, 1)

            pe.wait_ge(s_mlp, 16 * 3)
            layer1(0, 0, 1)
            layer2(0, 0)
            pe.wait_ge(s_in, 16 * 7)
            pe.wait_ge(s_init, S_H)
            pe.wait_ge(s_y2, 2)
            for b in range(BLOCKS):
                m = nc.tensor.matmul(ps[0:F, b // 4, (b % 4) * P:(b % 4 + 1) * P], h_in[:, b, :], ident_sb, start=True, stop=True)
                if b % 4 == 3 or b == BLOCKS - 1:
                    m.then_inc(s_ht, 1)
            pe.wait_ge(s_init, S_H + 1)
            pe.wait_ge(s_turned, 2)
            for c in range(BANKS):
                pe.wait_ge(s_htc, c + 1)
                n = min(4, BLOCKS - 4 * c)
                nc.tensor.matmul(ps[0:F, c, 0:n * P], wself_sb[:, :], agg_t[:, c * 512:c * 512 + n * P], start=True, stop=False)
                for k in range(n):
                    m = nc.tensor.matmul(ps[0:F, c, k * P:(k + 1) * P], x_turned[:, 4 * c + k, :], ident_sb,
                                         start=False, stop=(k == n - 1))
                m.then_inc(s_self, 1)
                if c == 4:
                    pe.wait_ge(s_check, 1)
                    nc.tensor.matmul(ps[0:1, 7, 0:1], checks[:, 5:6], checks[:, 6:7], start=True, stop=True).then_inc(s_verdict, 1)
            pe.wait_ge(s_selfc, BANKS)
            pe.wait_ge(s_b3rows, 16 * 6)

            def weights(g, slot, half, first_step):
                if not first_step:
                    pe.wait_ge(s_prod, 2 * g + half - 1)
                q = slice(64 * half, 64 * half + 64)
                for two in range(2):
                    pe.wait_ge(s_y2, 2 * g + two + 1)
                    nc.tensor.matmul(tpw_ps[:, half, two * 512:two * 512 + 512], ones_bf[q, :],
                                     b3_rows[q, :].unsqueeze(1).to_broadcast((64, 2, NTP)), start=True, stop=False)
                    for t in (2 * two, 2 * two + 1):
                        m = nc.tensor.matmul(tpw_ps[:, half, t * NTP:(t + 1) * NTP], y2[q, slot % 2, t * P:(t + 1) * P],
                                             w3_sb[q, :], start=False, stop=(t == 2 * two + 1))
                m.then_inc(s_tpw, 1)

            def count_pairs(g, half, first_step):
                pairs = (2 * half, 2 * half + 1)
                pe.wait_ge(s_lane, 2 * g + half + 1)
                pe.wait_ge(s_key, 2 * g + half + 1)
                for pair in pairs:
                    if not (first_step and pair < 2):
                        pe.wait_ge(s_stage, 4 * g + pair - 1)
                    for t in (2 * pair, 2 * pair + 1):
                        m = nc.tensor.matmul(cnt_ps[:, pair % 2, (t % 2) * KEYS:(t % 2 + 1) * KEYS],
                                             oh_a[:, half, t % TH, :], oh_k[:, half, t % TH, :], start=True, stop=True)
                    m.then_inc(s_cnt, 1)

            def aggregate(g, half):
                pe.wait_ge(s_msg, 2 * g + half + 1)
                pe.wait_ge(s_place, 2 * g + half + 1)
                if half == 0:
                    pe.wait_ge(s_aggadd, g + 1)
                for t in range(half * TH, half * TH + TH):
                    m = nc.tensor.matmul(agg_ps, oh_w[:, t, :], terms[:, t, :], start=(t == 0), stop=(t == TG - 1))
                m.then_inc(s_agg, 1)

            def turn(g):
                pe.wait_ge(s_aggred, g + 1)
                pe.sem_inc(s_turning, 1)
                nc.tensor.matmul(turn_ps, agg_sb[:, :], ident_w[:, :], start=True, stop=True).then_inc(s_turn, 1)

            def only_weights(g, slot, use, first_step, last):
                weights(g, slot, 0, first_step)
                if not last:
                    layer1(g + 1, (slot + 1) % 4, use + (slot == 3))
                weights(g, slot, 1, first_step)
                if not last:
                    layer2(g + 1, (slot + 1) % 4)

            def scatter(landed, done):
                def sum_rows(g, slot, use, first_step, last):
                    pe.wait_ge(landed[slot], use * (16 if landed is s_rows else 16 * TG))
                    for t in range(TG):
                        pe.wait_ge(s_all, done + TG * g + t + 1)
                        for b in range(BANKS):
                            m = nc.tensor.matmul(ps[0:F + 1, b, 0:BANK], rows[:, slot, t, :], oh_all[:, t % 2, b * BANK:(b + 1) * BANK],
                                                 start=(first_step and t == 0), stop=(last and t == TG - 1))
                        m.then_inc(s_scats, 1)
                every_group(pe, sum_rows)
                pe.wait_ge(s_scats, done + TILES)
                pe.sem_inc(s_scat, 1)

            def step(g, slot, use, first_step, last):
                weights(g, slot, 0, first_step)
                if not first_step:
                    aggregate(g - 1, 0)
                if not last:
                    layer1(g + 1, (slot + 1) % 4, use + (slot == 3))
                count_pairs(g, 0, first_step)
                weights(g, slot, 1, first_step)
                if not first_step:
                    aggregate(g - 1, 1)
                if not last:
                    layer2(g + 1, (slot + 1) % 4)
                count_pairs(g, 1, first_step)
                if not first_step:
                    turn(g - 1)

            with pe.If(dense(pe)):
                every_group(pe, step)
                aggregate(GROUPS - 1, 0)
                aggregate(GROUPS - 1, 1)
                turn(GROUPS - 1)
            with pe.Else():
                every_group(pe, only_weights)
                pe.wait_ge(s_prod, 2 * GROUPS)
                scatter(s_rows, 0)

            pe.wait_ge(s_layer0, 1)
            for half, (b0, b1) in enumerate(HALVES):
                for b in range(b0, b1):
                    m = nc.tensor.matmul(ps[:, half, (b - b0) * F:(b - b0 + 1) * F], agg_t[:, b * P:(b + 1) * P], perm_sb[:, :],
                                         start=True, stop=True)
                m.then_inc(s_x1, 1)
            with pe.If(dense(pe)):
                for part, (k0, k1) in enumerate(HALVES):
                    pe.wait_ge(s_parts, part + 1)
                    if part == 0:
                        pe.wait_ge(s_x1c, 2)
                    for b in (*range(BLOCKS - 2), BLOCKS - 1, BLOCKS - 2):
                        cols = min(P, ACOLS - b * P)
                        closes = part == 1 and (b % BB == BB - 1 or b == BLOCKS - 2)
                        for k in range(k0, k1):
                            m = nc.tensor.matmul(result_ps(b)[0:cols], counts[:, k, b * P:b * P + cols],
                                                 parts[:, k, :], start=(b % BB == 0 and k == 0),
                                                 stop=(closes and k == BLOCKS - 1))
                        if closes:
                            m.then_inc(s_fin, 1)
            with pe.Else():
                pe.wait_ge(s_x1c, 2)
                pe.wait_ge(s_parts, 2)
                scatter(s_grows, TILES)
                pe.wait_ge(s_sumst, 1)
                pe.wait_ge(s_spread, 16)
                for b in range(BLOCKS):
                    cols = min(P, ACOLS - b * P)
                    m = nc.tensor.matmul(result_ps(b)[0:cols], sums_t[:, b * P:b * P + cols], spread_sb, start=True, stop=True)
                    if b % BB == BB - 1 or b == BLOCKS - 1:
                        m.then_inc(s_fin, 1)

        @block.scalar
        def _(act):
            def root(variance_ready, count):
                act.wait_ge(variance_ready, count)
                nc.scalar.activation(stat[:, 1, :], stat[:, 3, :], ACT.Sqrt).then_inc(s_root, 1)

            def clear(first_row, end):
                n = (end - first_row) * ACOLS // 2
                return nc.scalar.copy(cleared(first_row, end), zero[:, :].to_broadcast((P, n)))

            def silu1(g, slot, first_step):
                act.wait_ge(s_l1, g + 1)
                if not first_step:
                    act.wait_ge(s_tpw, 2 * g - 2)
                nc.scalar.activation(y2[:, slot % 2, :], mlp_ps, ACT.Silu, bias=b12_sb[:, 0:1]).then_inc(s_y1, 1)

            def silu2(g, slot):
                act.wait_ge(s_l2, g + 1)
                for two in (slice(0, 256), slice(256, 512)):
                    nc.scalar.activation(y2[:, slot % 2, two], mlp_ps[:, two], ACT.Silu, bias=b12_sb[:, 1:2]).then_inc(s_y2, 1)

            act.wait_ge(s_zero, 1)
            clear(POOL_ROWS, POOL_ROWS + ACT_ROWS).then_inc(s_cleared, 1)
            act.wait_ge(s_x, 32)
            nc.scalar.copy(x_turned[:, :, 0:MUL], x_in[:, :, 0:MUL]).then_inc(s_turned, 1)
            nc.scalar.copy(x_turned[:, :, MUL:F].rearrange("p b (i w) -> p b i w", i=3),
                           x_in[:, :, MUL:F].rearrange("p b (w i) -> p b i w", i=3)).then_inc(s_turned, 1)
            root(s_init, S_VAR)
            act.wait_ge(s_mlp, 16 * 3)
            silu1(0, 0, True)
            silu2(0, 0)
            act.wait_ge(s_in, 16 * 7)
            for b in range(BANKS):
                act.wait_ge(s_ht, b + 1)
                n = min(4, BLOCKS - 4 * b) * P
                nc.scalar.copy(agg_t[:, b * 512:b * 512 + n], ps[0:F, b, 0:n]).then_inc(s_htc, 1)
            for c in range(BANKS):
                act.wait_ge(s_self, c + 1)
                n = min(4, BLOCKS - 4 * c) * P
                nc.scalar.copy(agg_t[:, c * 512:c * 512 + n], ps[0:F, c, 0:n]).then_inc(s_selfc, 1)

            def lanes(g, slot, half, first_step):
                act.wait_ge(s_cur, g + 1)
                if not first_step:
                    act.wait_ge(s_cnt, 4 * g + 2 * half - 2)
                for k in range(TH):
                    m = nc.scalar.activation(oh_a[:, half, k, :], iota_a[:, :], ACT.Abs, scale=-1.0,
                                             bias=cur[:, slot % 4, 0, half * TH + k:half * TH + k + 1])
                m.then_inc(s_dist, 1)
                act.wait_ge(s_dist, 2 * g + half + 1)
                nc.scalar.activation(oh_a[:, half, :, :], oh_a[:, half, :, :], ACT.Relu, scale=-1.0, bias=1.0).then_inc(s_lane, 1)

            def places(g, slot, half, first_step):
                act.wait_ge(s_cur, g + 1)
                if not first_step:
                    act.wait_ge(s_agg, 2 * g + half - 1)
                ts = slice(half * TH, half * TH + TH)
                for t in range(ts.start, ts.stop):
                    m = nc.scalar.activation(oh_w[:, t, :], iota_w[:, :], ACT.Abs, scale=-1.0, bias=cur[:, slot % 4, 2, t:t + 1])
                m.then_inc(s_far, 1)
                act.wait_ge(s_far, 2 * g + half + 1)
                nc.scalar.activation(oh_w[:, ts, :], oh_w[:, ts, :], ACT.Relu, scale=-1.0, bias=1.0).then_inc(s_place, 1)

            def copy_scalars(g, slot, use, first_step):
                act.wait_ge(s_gather[slot], 16 * TG * use)
                if not first_step:
                    act.wait_ge(s_prod, 2 * g - 1)
                nc.scalar.copy(lhs[:, slot % 2, :, 0:MUL], h_src[:, slot, :, 0:MUL]).then_inc(s_copied, 1)

            def unload(g, half, first_step):
                for pair in (2 * half, 2 * half + 1):
                    act.wait_ge(s_cnt, 4 * g + pair + 1)
                    if not (first_step and pair < 2):
                        act.wait_ge(s_addc, TG * g + 2 * pair - 2)
                    nc.scalar.copy(stage[:, pair % 2, :, :].rearrange("p a b -> p (a b)"), cnt_ps[:, pair % 2, :]).then_inc(s_stage, 1)

            def step(g, slot, use, first_step, last):
                if not last:
                    silu1(g + 1, (slot + 1) % 4, first_step)
                unload(g, 0, first_step)
                lanes(g, slot, 1, first_step)
                if not last:
                    silu2(g + 1, (slot + 1) % 4)
                places(g, slot, 0, first_step)
                if not last:
                    copy_scalars(g + 1, (slot + 1) % 4, use + (slot == 3), first_step)
                    lanes(g + 1, slot + 1, 0, False)
                unload(g, 1, first_step)
                places(g, slot, 1, first_step)

            copy_scalars(0, 0, 1, True)

            def only_silu(g, slot, use, first_step, last):
                if not last:
                    copy_scalars(g + 1, (slot + 1) % 4, use + (slot == 3), first_step)
                    silu1(g + 1, (slot + 1) % 4, first_step)
                    silu2(g + 1, (slot + 1) % 4)
                act.wait_ge(s_whole, g + 1)
                act.dma_start(msg_table[bass.ds(g, 1), :, :].rearrange("a p n -> (a p) n"),
                              msg[:, :, :].rearrange("p t f -> p (t f)")).then_inc(s_stored, 16)

            with act.If(dense(act)):
                lanes(0, 0, 0, True)
                every_group(act, step)
            with act.Else():
                every_group(act, only_silu)
                act.wait_ge(s_stored, 16 * GROUPS)
            for k, (b0, b1) in enumerate(HALVES):
                act.wait_ge(s_x1, k + 1)
                nc.scalar.copy(carve(work[:, :], b0 * F, (b1 - b0) * F), ps[:, k, 0:(b1 - b0) * F]).then_inc(s_x1c, 1)
            for k, (b0, b1) in enumerate(HALVES):
                act.wait_ge(s_mean, k * S_HALF + S_VAR - 1)
                nc.scalar.activation(stat[:, 1, b0:b1], stat[:, 3, b0:b1], ACT.Sqrt).then_inc(s_root, 1)

        @block.vector
        def _(dve):
            n_init = [0]

            def link(ins):
                n_init[0] += 1
                ins.then_inc(s_init, 1)
                dve.wait_ge(s_init, n_init[0])

            def layer_norm(of, to, xc, sq, step, root, b0, b1):
                def st(k):
                    return stat[:, k, b0:b1]

                def wide(k):
                    return st(k).unsqueeze(2).to_broadcast((P, b1 - b0, F))
                of, to, xc, sq = (a[:, b0:b1, :] for a in (of, to, xc, sq))
                step(nc.vector.tensor_reduce(st(0), of, X, ALU.add))
                step(nc.vector.tensor_scalar(st(1), st(0), 1.0 / F, None, ALU.mult))
                step(nc.vector.tensor_tensor(xc, of, wide(1), ALU.subtract))
                step(nc.vector.tensor_tensor(sq, xc, xc, ALU.mult))
                step(nc.vector.tensor_reduce(st(2), sq, X, ALU.add))
                step(nc.vector.tensor_scalar(st(3), st(2), 1.0 / F, EPS, ALU.mult, ALU.add))
                dve.wait_ge(s_root, root)
                step(nc.vector.reciprocal(st(0), st(1)))
                step(nc.vector.tensor_tensor(st(2), st(0), st(0), ALU.mult))
                step(nc.vector.tensor_tensor(st(2), st(2), st(3), ALU.mult))
                step(nc.vector.tensor_scalar(st(2), st(2), -0.5, 1.5, ALU.mult, ALU.add))
                step(nc.vector.tensor_tensor(st(0), st(0), st(2), ALU.mult))
                step(nc.vector.scalar_tensor_tensor(out=to, in0=xc, scalar=0.0, in1=wide(0), op0=ALU.max, op1=ALU.mult))

            link(nc.vector.memset(x_in[:, BLOCKS - 1:BLOCKS, :], 0.0))
            nc.vector.memset(zero[:, :], 0.0).then_inc(s_zero, 1)
            dve.wait_ge(s_zero, 1)
            nc.vector.memset(ones_bf[:, :], 1.0)
            nc.vector.memset(b3_rows[:, :], 0.0).then_inc(s_b3, 1)
            dve.wait_ge(s_x, 32)
            layer_norm(x_in, h_in, xc_in, sq_in, link, 1, 0, BLOCKS)
            dve.wait_ge(s_in, 16 * 7)
            nc.vector.tensor_scalar(w3_sb[:, 0:64], w3_sb[:, 0:64], C_MSG, None, ALU.mult)
            nc.vector.tensor_scalar(w3_sb[:, 64:128], w3_sb[:, 64:128], C_VEC, None, ALU.mult)
            nc.vector.tensor_scalar(w3_sb[:, 128:NTP], w3_sb[:, 128:NTP], C_MSG, None, ALU.mult)
            nc.vector.tensor_scalar(wself_sb[:, :], wself_sb[:, :], C_SELF, None, ALU.mult)
            nc.vector.tensor_scalar(b3_f[:, 1, 0:64], b3_f[:, 0, 0:64], C_MSG, None, ALU.mult)
            nc.vector.tensor_scalar(b3_f[:, 1, 64:128], b3_f[:, 0, 64:128], C_VEC, None, ALU.mult)
            link(nc.vector.tensor_scalar(b3_f[:, 1, 128:NTP], b3_f[:, 0, 128:NTP], C_MSG, None, ALU.mult))
            nc.vector.tensor_copy(b3_parts[:, 0, :], b3_f[:, 1, :]).then_inc(s_b3, 1)
            dve.wait_ge(s_b3, 2)
            link(nc.vector.tensor_tensor(b3_f[:, 0, :], b3_f[:, 1, :], b3_parts[:, 0, :], ALU.subtract))
            nc.vector.tensor_copy(b3_parts[:, 1, :], b3_f[:, 0, :]).then_inc(s_b3, 1)
            dve.wait_ge(s_b3, 3)
            nc.vector.tensor_tensor(b3_parts[:, 2, :], b3_f[:, 0, :], b3_parts[:, 1, :], ALU.subtract).then_inc(s_b3, 1)

            dve.wait_ge(s_edges, 48)
            link(nc.vector.tensor_scalar(scratch_i, src_all[:, :], P - 1, None, ALU.bitwise_and))
            link(nc.vector.tensor_copy(tables[:, 0, :], scratch_i))
            link(nc.vector.tensor_tensor(scratch_f, dst_all, first_bc, ALU.subtract))
            nc.vector.tensor_reduce(checks[:, 0:1], scratch_f, X, ALU.max)
            nc.vector.tensor_reduce(checks[:, 1:2], scratch_f, X, ALU.min)
            link(nc.vector.tensor_scalar(scratch_i, src_all[:, :], 7, 3, ALU.logical_shift_right, ALU.logical_shift_left))
            link(nc.vector.tensor_tensor(tables[:, 1, :], scratch_f, scratch_i, ALU.add))
            link(nc.vector.tensor_tensor(tables[:, 2, :].rearrange("p (g t) -> p g t", t=TG), dst_all.rearrange("p (g t) -> p g t", t=TG),
                                         first_bc.rearrange("p (g t) -> p g t", t=TG)[:, :, 0:1].to_broadcast((P, GROUPS, TG)), ALU.subtract))
            chk = checks[:, :]
            nc.vector.tensor_reduce(chk[:, 2:3], tables[:, 2:3, :], X, ALU.max)
            nc.vector.tensor_reduce(chk[:, 3:4], tables[:, 2:3, :], X, ALU.min)
            link(nc.vector.tensor_tensor(scratch_f[:, 0:TILES - SPAN + 1], first_bc[:, SPAN - 1:TILES],
                                         first_bc[:, 0:TILES - SPAN + 1], ALU.subtract))
            link(nc.vector.tensor_reduce(chk[:, 4:5], scratch_f[:, 0:TILES - SPAN + 1], X, ALU.min))
            for k, (op, bound) in enumerate(((ALU.is_le, WT - 1), (ALU.is_ge, 0), (ALU.is_le, WG - 1), (ALU.is_ge, 0), (ALU.is_ge, 1))):
                nc.vector.tensor_scalar(chk[:, k:k + 1], chk[:, k:k + 1], float(bound), None, op)
            link(nc.vector.memset(chk[:, 6:7], 1.0))
            nc.vector.tensor_reduce(chk[:, 5:6], chk[:, 0:5], X, ALU.min).then_inc(s_check, 1)
            nc.vector.tensor_copy(cleared(POOL_ROWS + ACT_ROWS, EARLY),
                                  zero[:, :].to_broadcast((P, (EARLY - POOL_ROWS - ACT_ROWS) * ACOLS // 2))).then_inc(s_cleared, 1)
            dve.wait_ge(s_verdict, 1)
            nc.vector.tensor_scalar(dense_sb[:, :], ps[0:1, 7, 0:1], P - 0.5, None, ALU.is_ge).then_inc(s_dense, 1)
            dve.wait_ge(s_htab, 16)
            dve.wait_ge(s_b3rows, 16 * 6)
            dve.wait_ge(s_b3, 4)
            dve.wait_ge(s_iota, 3)

            def current(g, slot):
                nc.vector.tensor_copy(cur[:, slot % 4, :, :], tables[:, :, bass.ds(g * TG, TG)]).then_inc(s_cur, 1)

            def keys(g, slot, half, first_step):
                dve.wait_ge(s_cur, g + 1)
                if not first_step:
                    dve.wait_ge(s_cnt, 4 * g + 2 * half - 2)
                for k in range(TH):
                    t = half * TH + k
                    m = nc.vector.tensor_scalar(oh_k[:, half, k, :], iota_k[:, :], cur[:, slot % 4, 1, t:t + 1], None, ALU.is_equal)
                m.then_inc(s_key, 1)

            def dots(g, slot, first_step):
                dve.wait_ge(s_product, g + 1)
                if not first_step:
                    dve.wait_ge(s_prod, 2 * g - 2)
                nc.vector.tensor_reduce(lhs[:, slot % 2, :, MUL:2 * MUL], hv_sh1[:, :, :, :], X, ALU.add).then_inc(s_dot, 1)

            def products(g, slot, half, first_step, between, messages_used=True):
                ts = slice(half * TH, half * TH + TH)
                w = tpw_ps[:, half, :].rearrange("p (t n) -> p t n", n=NTP)
                if half == 0:
                    dve.wait_ge(s_dot, g + 1)
                    dve.wait_ge(s_prep, g + 1)
                    dve.wait_ge(s_copied, g + 1)
                dve.wait_ge(s_tpw, 2 * g + half + 1)
                if not (first_step and half == 0):
                    dve.wait_ge(s_sum, 2 * g + half)
                nc.vector.tensor_tensor(prod_s.rearrange("p t (u w) -> p t u w", w=MUL),
                                        w[:, :, 0:192].rearrange("p t (u w) -> p t u w", w=MUL),
                                        lhs[:, slot % 2, ts, 0:3 * MUL].unsqueeze(3).to_broadcast((P, TH, 24, MUL)), ALU.mult)
                between(0)
                if messages_used and not first_step:
                    dve.wait_ge(s_agg, 2 * g + half - 1)
                for i in range(3):
                    m = nc.vector.tensor_tensor(vec_terms[:, ts, i, 0:64].rearrange("p t (u w) -> p t u w", w=MUL),
                                                w[:, :, 192:256].rearrange("p t (u w) -> p t u w", w=MUL),
                                                lhs_v[:, slot % 2, ts, i, :].unsqueeze(3).to_broadcast((P, TH, MUL, MUL)), ALU.mult)
                    if i < 2:
                        between(i + 1)
                m.then_inc(s_prod, 1)
                between(3)

            def scalar_sums(g, half):
                ts = slice(half * TH, half * TH + TH)
                dve.wait_ge(s_prod, 2 * g + half + 1)
                nc.vector.tensor_reduce(t01[:, :, :], prod_s[:, :, 0:64].rearrange("p t (u w) -> p t w u", w=MUL), X, ALU.add).then_inc(s_t01, 1)
                nc.vector.tensor_reduce(terms[:, ts, VEC:MV], prod_s[:, :, 64:192].rearrange("p t (u w) -> p t w u", w=MUL), X, ALU.add).then_inc(s_sum, 1)

            def vector_part(g, slot, half):
                ts = slice(half * TH, half * TH + TH)
                dve.wait_ge(s_t01, 2 * g + half + 1)
                nc.vector.tensor_tensor(vec_terms[:, ts, :, 64:72], t01[:, :, :].unsqueeze(2).to_broadcast((P, TH, 3, MUL)),
                                        sh_sb[:, slot, ts, 1:4].unsqueeze(3).to_broadcast((P, TH, 3, MUL)), ALU.mult).then_inc(s_msg, 1)

            def add_count(g, t, base):
                dve.wait_ge(s_stage, 4 * g + t // 2 + 1)
                dve.wait_ge(s_addc, TG * g + t)
                to = counts[:, :, bass.ds(base, WT)]
                nc.vector.tensor_tensor(to, to, stage[:, t // 2 % 2, t % 2, :].rearrange("p (b w) -> p b w", w=WT), ALU.add).then_inc(s_addc, 1)

            def reduce_aggregate(g):
                dve.wait_ge(s_agg, 2 * g + 2)
                nc.vector.tensor_copy(agg_sb[:, 0:MUL], agg_ps[:, VEC:MV])
                nc.vector.tensor_reduce(agg_sb[:, MUL:F].rearrange("p (i w) -> p i w", i=3),
                                        agg_ps[:, 0:VEC].rearrange("p (i u w) -> p i w u", i=3, u=US), X, ALU.add).then_inc(s_aggred, 1)

            def add_aggregate(g, base):
                dve.wait_ge(s_turn, g + 1)
                dve.wait_ge(s_aggadd, g + 1)
                to = agg_t[:, bass.ds(base, WG)]
                nc.vector.tensor_tensor(to, to, turn_ps, ALU.add).then_inc(s_aggadd, 1)

            def bases_of(tile, n):
                return nc.values_load_multi_w_load_instructions(
                    first_sb[0:1, bass.ds(tile, n)], engines=[mybir.EngineType.DVE], min_val=0, max_val=N,
                    skip_runtime_bounds_check_because="destinations are node numbers, and the padding's is N")[1]

            def nothing(k):
                pass

            def step(g, slot, use, first_step, last):
                if first_step:
                    late, now, before = nothing, bases_of(0, TH), None
                else:
                    bases = bases_of(TG * g - TG, TG + TH)
                    late, now, before = bases[TH:TG], bases[TG:], bases[0]
                if not last:
                    if not first_step:
                        dve.wait_ge(s_lane, 2 * g - 1)
                        dve.wait_ge(s_place, 2 * g - 1)
                    current(g + 1, slot + 1)
                products(g, slot, 0, first_step, nothing if first_step else lambda k: add_count(g - 1, TH + k, late[k]))
                keys(g, slot, 1, first_step)
                scalar_sums(g, 0)
                vector_part(g, slot, 0)

                def others(k):
                    add_count(g, k, now[k])
                    if k == 0 and not first_step:
                        reduce_aggregate(g - 1)
                products(g, slot, 1, first_step, others)
                if not last:
                    keys(g + 1, slot + 1, 0, False)
                if not last:
                    dots(g + 1, slot + 1, first_step)
                if not first_step:
                    add_aggregate(g - 1, before)
                scalar_sums(g, 1)
                vector_part(g, slot, 1)

            def only_messages(g, slot, use, first_step, last):
                if not first_step:
                    dve.wait_ge(s_whole, g)
                for half in range(2):
                    if half == 1 and not last:
                        dots(g + 1, slot + 1, first_step)
                    products(g, slot, half, first_step, nothing, False)
                    scalar_sums(g, half)
                    vector_part(g, slot, half)
                dve.wait_ge(s_msg, 2 * g + 2)
                dve.wait_ge(s_sum, 2 * g + 2)
                if not first_step:
                    dve.wait_ge(s_stored, 16 * g)
                nc.vector.tensor_copy(msg[:, :, 0:MUL], terms[:, :, VEC:MV])
                for i in range(3):
                    m = nc.vector.tensor_reduce(msg[:, :, MUL + i * MUL:2 * MUL + i * MUL],
                                                vec_terms[:, :, i, :].rearrange("p t (u w) -> p t w u", u=US), X, ALU.add)
                m.then_inc(s_whole, 1)

            def all_places(done):
                def tiles(g, slot, use, first_step, last):
                    dve.wait_ge(s_all, done + TG * g)
                    nc.vector.tensor_copy(cur[:, 0, 0, :], dst_all[:, bass.ds(g * TG, TG)]).then_inc(s_cur, 1)
                    dve.wait_ge(s_cur, done // TG + g + 1)
                    for t in range(TG):
                        if not (first_step and t < 2):
                            dve.wait_ge(s_scats, done + TG * g + t - 1)
                        nc.vector.tensor_scalar(oh_all[:, t % 2, :], iota_all, cur[:, 0, 0, t:t + 1], None, ALU.is_equal).then_inc(s_all, 1)
                every_group(dve, tiles)

            with dve.If(dense(dve)):
                dve.wait_ge(s_dense, 1)
                dve.wait_ge(s_turned, 2)
                dve.wait_ge(s_ht, BANKS)
                split, end = 5 * TILES + 4 * NF, (BLOCKS - EARLY) * ACOLS // 2
                nc.vector.tensor_copy(early[:, 0:split], zero[:, :].to_broadcast((P, split)))
                dve.wait_ge(s_self, BANKS)
                nc.vector.tensor_copy(early[:, split:], zero[:, :].to_broadcast((P, end - split))).then_inc(s_cleared, 1)
                dve.wait_ge(s_cleared, 4)
                dve.sem_inc(s_aggadd, 1)
                current(0, 0)
                keys(0, 0, 0, True)
                dots(0, 0, True)
                every_group(dve, step)
                bases = bases_of(TILES - TG, TG)
                for t in range(TH, TG):
                    add_count(GROUPS - 1, t, bases[t])
                reduce_aggregate(GROUPS - 1)
                add_aggregate(GROUPS - 1, bases[0])
                dve.wait_ge(s_aggadd, GROUPS + 1)
            with dve.Else():
                dve.wait_ge(s_cleared, 3)
                dots(0, 0, True)
                every_group(dve, only_messages)
                dve.wait_ge(s_prep, GROUPS)
                nc.vector.memset(rows[:, :, :, F:F + 1], 1.0).then_inc(s_ready, 1)
                dve.wait_ge(s_alliota, 1)
                all_places(0)
                dve.wait_ge(s_scat, 1)
                for b in range(BANKS):
                    m = nc.vector.tensor_tensor(agg_t[:, b * BANK:(b + 1) * BANK], agg_t[:, b * BANK:(b + 1) * BANK],
                                                ps[0:F, b, 0:BANK], ALU.add)
                m.then_inc(s_aggadd, 1)
                dve.wait_ge(s_aggadd, 1)
            dve.sem_inc(s_layer0, 1)

            n_fin = [0]

            def then(ins):
                n_fin[0] += 1
                ins.then_inc(s_mean, 1)
                dve.wait_ge(s_mean, n_fin[0])
            nc.vector.memset(parts[:, :, 2 * F:PARTS], 1.0)
            for k, (b0, b1) in enumerate(HALVES):
                dve.wait_ge(s_x1c, k + 1)
                layer_norm(x_1, h_1, xc_1, sq_1, then, k + 2, b0, b1)
                dve.sem_inc(s_h1, 1)
                then(nc.vector.tensor_copy(parts[:, b0:b1, 0:F], h_1[:, b0:b1, :]))
                then(nc.vector.tensor_tensor(xc_1[:, b0:b1, :], h_1[:, b0:b1, :], parts[:, b0:b1, 0:F], ALU.subtract))
                nc.vector.tensor_scalar(parts[:, b0:b1, F:2 * F], xc_1[:, b0:b1, :], LOW, None, ALU.mult).then_inc(s_parts, 1)
            with dve.If(general(dve)):
                all_places(TILES)
                dve.wait_ge(s_scat, 2)
                dve.wait_ge(s_parts, 2)
                for b in range(BANKS):
                    m = nc.vector.tensor_copy(sums_t[:, b * BANK:(b + 1) * BANK], ps[0:F + 1, b, 0:BANK])
                m.then_inc(s_sumst, 1)
            for bank, b0 in enumerate(range(0, BLOCKS, BB)):
                b1 = min(b0 + BB, BLOCKS)
                dve.wait_ge(s_fin, bank + 1)
                v = ps[:, bank, 0:(b1 - b0) * PARTS].rearrange("p (b f) -> p b f", f=PARTS)
                of, mean = stat[:, 0, b0:b1], stat[:, 1, b0:b1]
                nc.vector.tensor_scalar(xc_1[:, b0:b1, :], v[:, :, F:2 * F], 1.0 / LOW, None, ALU.mult)
                then(nc.vector.tensor_scalar(of.unsqueeze(2), v[:, :, 2 * F:PARTS], 1.0, None, ALU.max))
                nc.vector.reciprocal(mean, of)
                then(nc.vector.tensor_tensor(h_1[:, b0:b1, :], xc_1[:, b0:b1, :], v[:, :, 0:F], ALU.add))
                then(nc.vector.tensor_tensor(h_1[:, b0:b1, :], h_1[:, b0:b1, :], mean.unsqueeze(2).to_broadcast((P, b1 - b0, F)), ALU.mult))
                nc.vector.tensor_tensor(h_1[:, b0:b1, :], h_1[:, b0:b1, :], x_1[:, b0:b1, :], ALU.add).then_inc(s_res, 1)


def kernel(x, src, dst, edge_attr_4, edge_attr_8, L0_gnn_W1, L0_gnn_b1, L0_gnn_W2, L0_gnn_b2, L0_gnn_W3, L0_gnn_b3,
           L0_gnn_Ws, L0_gnn_Wv):
    import numpy as np
    import concourse.bacc as bacc
    from concourse.bass_utils import run_bass_kernel_spmd

    f32, i32 = np.float32, np.int32
    padded = TILES * P

    def pad(a, fill=0):
        a = np.asarray(a)
        to = np.full((padded,) + a.shape[1:], fill, a.dtype)
        to[:E] = a
        return to

    src_p = np.ascontiguousarray(pad(src).reshape(TILES, P).T)
    dst_p = np.ascontiguousarray(pad(dst, N).reshape(TILES, P).T)
    sh_p = np.ascontiguousarray(pad(edge_attr_4).reshape(GROUPS, TG, P, 4).transpose(0, 2, 1, 3).reshape(GROUPS, P, TG * 4))
    rad_p = np.ascontiguousarray(pad(edge_attr_8).reshape(GROUPS, 2, TH * P, NB).transpose(0, 1, 3, 2).reshape(GROUPS, 2 * NB, TH * P))

    def in_order(a):
        return np.concatenate([a[:, 128:192], a[:, 64:128], a[:, 0:64], a[:, 192:]], axis=1)
    w1 = np.zeros((2 * NB, P), f32)
    w2 = np.zeros((P, P), f32)
    w3 = np.zeros((P, NTP), f32)
    b12 = np.zeros((P, 2), f32)
    for k in range(2):
        w1[k * NB:(k + 1) * NB, k * HR:(k + 1) * HR] = L0_gnn_W1
        w2[k * HR:(k + 1) * HR, k * HR:(k + 1) * HR] = L0_gnn_W2
        w3[k * HR:(k + 1) * HR] = in_order(np.asarray(L0_gnn_W3))
        b12[k * HR:(k + 1) * HR, 0] = L0_gnn_b1
        b12[k * HR:(k + 1) * HR, 1] = L0_gnn_b2
    wself = np.zeros((F, F), f32)
    perm = np.zeros((F, F), f32)
    wself[0:MUL, 0:MUL] = L0_gnn_Ws
    perm[range(MUL), range(MUL)] = 1
    for i in range(3):
        wself[MUL + i:F:3, MUL + i * MUL:MUL + (i + 1) * MUL] = L0_gnn_Wv
        perm[range(MUL + i * MUL, MUL + (i + 1) * MUL), range(MUL + i, F, 3)] = 1
    spread = np.zeros((F + 1, PARTS), f32)
    spread[range(F), range(F)] = 1
    spread[F, 2 * F] = 1
    arrays = {
        "x": np.asarray(x), "src": src_p, "dst": dst_p, "first": np.ascontiguousarray(dst_p[0:1, :]), "sh": sh_p, "rad": rad_p,
        "w1": w1, "w2": w2, "w3": w3, "bias12": b12, "b3": in_order(np.asarray(L0_gnn_b3).reshape(1, NTP)), "wself": wself,
        "perm": perm, "ident": np.eye(P, dtype=f32), "spread": spread,
    }
    nc = bacc.Bacc("TRN2", target_bir_lowering=False, num_devices=1)
    args = [nc.dram_tensor(n, a.shape, mybir.dt.from_np(a.dtype), kind="ExternalInput").ap() for n, a in arrays.items()]
    out = nc.dram_tensor("out_0", (N, F), F32, kind="ExternalOutput").ap()
    build(nc, *args, out)
    return run_bass_kernel_spmd(nc, [arrays], core_ids=[0]).results[0]["out_0"]
```

```python
from contextlib import ExitStack

import concourse.bass as bass
from concourse import mybir

F32 = mybir.dt.float32
BF16 = mybir.dt.bfloat16
FP16 = mybir.dt.float16
I32 = mybir.dt.int32
ALU = mybir.AluOpType
ACT = mybir.ActivationFunctionType
X = mybir.AxisListType.X

P = 128
N, F, E = 3125, 32, 103125
MUL, HR, NB = 8, 64, 8
NTP = 4 * MUL * MUL
TG = 8
TH = TG // 2
GROUPS = -(-E // (TG * P))
TILES = GROUPS * TG
BLOCKS = -(-N // P)
LAST = N - (BLOCKS - 1) * P
WT = 8
WG = 64
US = MUL + 1
VEC = 3 * US * MUL
MV = VEC + MUL
KEYS = BLOCKS * WT
COLS = BLOCKS * P
ACOLS = 3136
NF = BLOCKS * F
SPAN = 16
BANKS, BANK = 7, ACOLS // 7
PARTS = 2 * F + 1
BB = 7
HALVES = ((0, 9), (9, BLOCKS))
LOW = 2048.0
POOL_ROWS, ACT_ROWS = 11, 2
EARLY = 19
EARLY_WORDS = (BLOCKS - EARLY) * ACOLS // 2
INPUTS = 5 * TILES + 4 * NF
EPS = 1e-5
C_MSG = (2.0 * MUL) ** -0.5 / 16.0 ** 0.5
C_VEC = C_MSG / 3.0 ** 0.5
C_SELF = MUL ** -0.5


def build(nc, x, src, dst, first, sh, rad, w1, w2, w3, bias12, b3, wself, ident, spread, out):
    h_table = nc.dram_tensor("h_table", (COLS, F), F32, kind="Internal").ap()
    msg_table = nc.dram_tensor("msg_table", (GROUPS, P, TG * F), F32, kind="Internal").ap()
    ctx = ExitStack()
    with ctx:
        def sb(name, shape, dt):
            return ctx.enter_context(nc.sbuf_tensor(name, shape, dt))

        def sem(name):
            return ctx.enter_context(nc.semaphore(name))

        ps = ctx.enter_context(nc.psum_tensor("ps", [P, 8, 512], F32))
        mlp_ps = ps[:, 0, :]
        tpw_ps = ps[:, 1:5, :].rearrange("p (h b) n -> p h (b n)", h=2)
        cnt_ps = ps[:, 5:7, 0:2 * KEYS]
        agg_ps = ps[0:WG, 7, 0:MV]
        turn_ps = ps[0:F, 7, 256:256 + WG]

        counts = sb("counts", [P, BLOCKS, ACOLS], FP16)
        packed = sb("packed", [P, COLS], F32)
        agg_t = packed[0:F, :]
        rad_sb = packed[32:32 + 2 * NB, 0:2048].rearrange("p (s n) -> p s n", s=4)
        w1_sb = packed[32:32 + 2 * NB, 2048:2048 + P]
        first_sb = packed[64:65, 0:TILES].bitcast(I32)
        tables = sb("tables", [P, 3, TILES], FP16)
        stat = sb("stat", [P, 4, BLOCKS], F32)
        zero = sb("zero", [P, 1], F32)
        checks = sb("checks", [P, 8], F32)
        dense_sb = sb("dense_sb", [1, 1], I32)
        w2_sb = sb("w2_sb", [P, P], F32)
        w3_sb = sb("w3_sb", [P, NTP], F32)
        b12_sb = sb("b12_sb", [P, 2], F32)
        b3_rows = sb("b3_rows", [P, NTP], BF16)
        ones_bf = sb("ones_bf", [P, P], BF16)
        wself_sb = sb("wself_sb", [F, F], F32)
        iota_a = sb("iota_a", [P, P], FP16)
        iota_k = sb("iota_k", [P, KEYS], FP16)
        iota_w = sb("iota_w", [P, WG], F32)

        sh_sb = sb("sh_sb", [P, 4, TG, 4], F32)
        idx_sb = sb("idx_sb", [P, 4, TG], I32)
        h_src = sb("h_src", [P, 4, TG, F], F32)
        y2 = sb("y2", [P, 2, 512], F32)
        lhs = sb("lhs", [P, 2, TG, 2 * MUL + F], F32)
        lhs_v = lhs[:, :, :, 3 * MUL:].rearrange("p s t (u i) -> p s t i u", i=3)
        hv_sh1 = sb("hv_sh1", [P, TG, MUL, 3], F32)
        cur = sb("cur", [P, 4, 3, TG], F32)
        hot = sb("hot", [P, TH * P + TH * KEYS + TG * WG], F32)
        oh_a = hot[:, 0:TH * P].bitcast(FP16).rearrange("p (s t n) -> p s t n", s=2, t=TH)
        oh_k = hot[:, TH * P:TH * (P + KEYS)].bitcast(FP16).rearrange("p (s t n) -> p s t n", s=2, t=TH)
        oh_w = hot[:, TH * (P + KEYS):].rearrange("p (t n) -> p t n", t=TG)
        work = sb("work", [P, TH * 192 + TG * MV], F32)
        prod_s = work[:, 0:TH * 192].rearrange("p (t n) -> p t n", t=TH)
        terms = work[:, TH * 192:].rearrange("p (t n) -> p t n", t=TG)
        vec_terms = terms[:, :, 0:VEC].rearrange("p t (i n) -> p t i n", i=3)
        t01 = sb("t01", [P, TH, MUL], F32)
        agg_sb = sb("agg_sb", [WG, F], F32)
        ident_w = sb("ident_w", [WG, WG], F32)
        stage = sb("stage", [P, 2, 2, KEYS], FP16)

        early = counts[:, EARLY:BLOCKS, :].rearrange("p a b -> p (a b)").bitcast(F32)

        def carve(flat, start, n):
            return flat[:, start:start + n]

        def own(lead, n):
            lead[0] += n
            return early[:, lead[0] - n:lead[0]]

        def cleared(first_row, end):
            return counts[:, first_row:end, :].rearrange("p a b -> p (a b)").bitcast(F32)

        def nodes(flat):
            return flat.rearrange("p (b f) -> p b f", f=F)

        given = [0]
        src_all, dst_all, first_bc, scratch_i = (own(given, TILES).bitcast(I32) for _ in range(4))
        scratch_f = own(given, TILES)
        x_in, h_in, xc_in, sq_in = (nodes(own(given, NF)) for _ in range(4))
        ident_sb = own(given, P)
        b3_f = own(given, 2 * NTP)[0:1, :].rearrange("p (a n) -> p a n", a=2)
        b3_parts = own(given, 3 * NTP // 2)[0:1, :].bitcast(BF16).rearrange("p (a n) -> p a n", a=3)
        x_turned = nodes(own(given, NF))
        free = counts[:, 0:EARLY, :].rearrange("p a b -> p (a b)").bitcast(F32)
        iota_all = free[:, 0:ACOLS]
        oh_all = free[:, ACOLS:3 * ACOLS].rearrange("p (s n) -> p s n", s=2)
        rows = free[:, 3 * ACOLS:3 * ACOLS + 4 * TG * (F + 1)].rearrange("p (s t f) -> p s t f", s=4, t=TG)
        msg = free[:, 4 * ACOLS - TG * F:4 * ACOLS].rearrange("p (t f) -> p t f", t=TG)
        sums_t = free[0:F + 1, 4 * ACOLS:5 * ACOLS]
        spread_sb = free[0:F + 1, 5 * ACOLS:5 * ACOLS + PARTS]
        x_1, h_1, xc_1 = (nodes(carve(work[:, :], k * NF, NF)) for k in range(3))
        sq_1 = nodes(y2[:, :, :].rearrange("p a b -> p (a b)")[:, 0:NF])
        parts = hot.bitcast(FP16)[:, 0:BLOCKS * PARTS].rearrange("p (b f) -> p b f", f=PARTS)

        weights_landed = sem("weights_landed")
        mlp_landed = sem("mlp_landed")
        x_landed = sem("x_landed")
        zero_ready = sem("zero_ready")
        x_turned_ready = sem("x_turned_ready")
        root_ready = sem("root_ready")
        edges_landed = sem("edges_landed")
        preamble_step = sem("preamble_step")
        iotas_ready = sem("iotas_ready")
        b3_step = sem("b3_step")
        b3_rows_landed = sem("b3_rows_landed")
        h_stored = sem("h_stored")
        h_turned = sem("h_turned")
        h_t_copied = sem("h_t_copied")
        self_ready = sem("self_ready")
        self_copied = sem("self_copied")
        rad_landed = [sem(f"rad_landed{k}") for k in range(4)]
        sh_landed = [sem(f"sh_landed{k}") for k in range(4)]
        sources_landed = [sem(f"sources_landed{k}") for k in range(4)]
        idx_landed = [sem(f"idx_landed{k}") for k in range(4)]
        hv_sh1_ready = sem("hv_sh1_ready")
        dots_ready = sem("dots_ready")
        scaled_ready = sem("scaled_ready")
        scalars_copied = sem("scalars_copied")
        layer1_ready = sem("layer1_ready")
        silu1_ready = sem("silu1_ready")
        layer2_ready = sem("layer2_ready")
        silu2_ready = sem("silu2_ready")
        weights_ready = sem("weights_ready")
        products_ready = sem("products_ready")
        t01_ready = sem("t01_ready")
        scalars_summed = sem("scalars_summed")
        terms_ready = sem("terms_ready")
        messages_ready = sem("messages_ready")
        current_ready = sem("current_ready")
        lane_distances_ready = sem("lane_distances_ready")
        place_distances_ready = sem("place_distances_ready")
        lanes_ready = sem("lanes_ready")
        keys_ready = sem("keys_ready")
        places_ready = sem("places_ready")
        counts_ready = sem("counts_ready")
        counts_staged = sem("counts_staged")
        counts_added = sem("counts_added")
        half_aggregated = sem("half_aggregated")
        aggregate_reduced = sem("aggregate_reduced")
        turn_starts = sem("turn_starts")
        aggregate_turned = sem("aggregate_turned")
        aggregate_added = sem("aggregate_added")
        x1_ready = sem("x1_ready")
        x1_copied = sem("x1_copied")
        h1_ready = sem("h1_ready")
        parts_ready = sem("parts_ready")
        sums_ready = sem("sums_ready")
        second_step = sem("second_step")
        result_ready = sem("result_ready")
        result_stored = sem("result_stored")
        checks_ready = sem("checks_ready")
        verdict_ready = sem("verdict_ready")
        dense_ready = sem("dense_ready")
        rows_cleared = sem("rows_cleared")
        layer0_done = sem("layer0_done")
        messages_stored = sem("messages_stored")
        ones_ready = sem("ones_ready")
        iota_all_ready = sem("iota_all_ready")
        hot_tile_ready = sem("hot_tile_ready")
        rows_landed = [sem(f"rows_landed{k}") for k in range(4)]
        idx_copied = sem("idx_copied")
        sources_again_landed = [sem(f"sources_again_landed{k}") for k in range(4)]
        tile_summed = sem("tile_summed")
        all_summed = sem("all_summed")
        sums_copied = sem("sums_copied")
        spread_landed = sem("spread_landed")
        gathers_start = sem("gathers_start")
        block = ctx.enter_context(nc.Block())

        def result_ps(b):
            return ps[:, b // BB, (b % BB) * PARTS:(b % BB + 1) * PARTS]

        VARIANCE_STEP = 7
        H_STEP = 13
        HALF_STEPS = 14

        def every_group(eng, step):
            step(0, 0, 1, True, False)
            rounds = (GROUPS - 2) // 4
            with eng.Fori(0, rounds) as i:
                for k in range(1, 5):
                    step(4 * i + k, k % 4, i + 1 + k // 4, False, False)
            for g in range(4 * rounds + 1, GROUPS):
                step(g, g % 4, g // 4 + 1, False, g == GROUPS - 1)

        def dense(eng):
            eng.wait_ge(dense_ready, 1)
            return nc.values_load(dense_sb[0:1, 0:1], engines=[eng.engine], min_val=0, max_val=1,
                                  skip_runtime_bounds_check_because="a comparison's result")

        def general(eng):
            return 1 - dense(eng)

        def fetch_groups(eng, step):
            for k in range(4):
                step(k, k, 1, True, False)
            rounds = (GROUPS - 5) // 4
            with eng.Fori(0, rounds) as i:
                for k in range(4):
                    step(4 * i + 4 + k, k, i + 2, False, False)
            for g in range(4 * rounds + 4, GROUPS):
                step(g, g % 4, g // 4 + 1, False, g == GROUPS - 1)

        @block.sync
        def _(sp):
            full = BLOCKS - 1

            def load(g, slot, wait):
                if wait:
                    sp.wait_ge(layer1_ready, g - 3)
                    sp.wait_ge(scaled_ready, g - 3)
                    sp.wait_ge(terms_ready, 2 * g - 6)
                sp.dma_start(rad_sb[:, slot, :], rad[bass.ds(g, 1), :, :].rearrange("a p n -> (a p) n")
                             ).then_inc(rad_landed[slot], 16)
                sp.dma_start(idx_sb[:, slot, :], src[:, bass.ds(g * TG, TG)]).then_inc(idx_landed[slot], 16)
                sp.dma_start(sh_sb[:, slot, :, :], sh[bass.ds(g, 1), :, :].rearrange("a p (t c) -> (a p) t c", c=4)
                             ).then_inc(sh_landed[slot], 16)

            sp.wait_ge(preamble_step, 1)
            sp.dma_start(x_in[:, 0:full, :], x[0:full * P, :].rearrange("(b p) f -> p b f", p=P)).then_inc(x_landed, 16)
            sp.dma_start(x_in[0:LAST, full, :], x[full * P:N, :]).then_inc(x_landed, 16)
            for to, fr in ((w1_sb, w1), (b12_sb[:, :], bias12), (w2_sb[:, :], w2)):
                sp.dma_start(to, fr).then_inc(mlp_landed, 16)
            load(0, 0, False)
            for to, fr in ((ident_sb, ident), (w3_sb[:, :], w3), (wself_sb[:, :], wself), (ident_w[:, :], ident[0:WG, 0:WG])):
                sp.dma_start(to, fr).then_inc(weights_landed, 16)
            sp.dma_start(b3_f[:, 0, :], b3).then_inc(weights_landed, 16)
            sp.dma_start(first_sb, first).then_inc(weights_landed, 16)
            sp.dma_start(src_all, src).then_inc(edges_landed, 16)
            sp.dma_start(dst_all, dst).then_inc(edges_landed, 16)
            sp.dma_start(first_bc, first.partition_broadcast(P)).then_inc(edges_landed, 16)
            load(1, 1, False)
            sp.wait_ge(preamble_step, H_STEP)
            sp.dma_start(h_table.rearrange("(b p) f -> p b f", p=P), h_in).then_inc(h_stored, 16)
            load(2, 2, False)
            load(3, 3, False)
            sp.wait_ge(b3_step, 4)
            for half in range(2):
                for j in range(3):
                    sp.dma_start(b3_rows[64 * half + j:64 * half + j + 1, :], b3_parts[:, j, :]).then_inc(b3_rows_landed, 16)

            def loads(g, slot, use, first_step, last):
                load(g + 4, slot, True)
            loads(0, 0, 1, True, False)
            rounds = (GROUPS - 6) // 4
            with sp.Fori(0, rounds) as i:
                for k in range(1, 5):
                    loads(4 * i + k, k % 4, i + 1, False, False)
            for g in range(4 * rounds + 1, GROUPS - 4):
                loads(g, g % 4, 1, False, True)
            with sp.If(general(sp)):
                sp.wait_ge(messages_stored, 16 * GROUPS)
                sp.wait_ge(ones_ready, 1)

                def fetch(g, slot, use, first_step, last):
                    if not first_step:
                        sp.wait_ge(tile_summed, TG * g - 3 * TG)
                    sp.dma_start(rows[:, slot, :, 0:F], msg_table[bass.ds(g, 1), :, :].rearrange("a p (t f) -> (a p) t f", f=F)
                                 ).then_inc(rows_landed[slot], 16)
                fetch_groups(sp, fetch)
                sp.dma_start(spread_sb, spread).then_inc(spread_landed, 16)
                sp.wait_ge(h1_ready, 2)
                sp.dma_start(h_table.rearrange("(b p) f -> p b f", p=P), h_1).then_inc(h_stored, 16)
            for k, b in enumerate(range(0, full, BB)):
                sp.wait_ge(result_ready, k + 1)
                n = min(BB, full - b)
                sp.dma_start(out[b * P:(b + n) * P, :].rearrange("(b p) f -> p b f", p=P), h_1[:, b:b + n, :]
                             ).then_inc(result_stored, 16)
            sp.dma_start(out[full * P:N, :], h_1[0:LAST, full, :]).then_inc(result_stored, 16)
            sp.wait_ge(result_stored, 16 * (-(-full // BB) + 1))
            sp.wait_ge(h_stored, 16)

        @block.gpsimd
        def _(pool):
            for to, n in ((iota_a, P), (iota_k, KEYS), (iota_w, WG)):
                nc.gpsimd.iota(to[:, :], pattern=[[1, n]], base=0, channel_multiplier=0,
                               allow_small_or_imprecise_dtypes=True).then_inc(iotas_ready, 1)
            nc.gpsimd.memset(cleared(0, POOL_ROWS), 0.0).then_inc(rows_cleared, 1)
            pool.wait_ge(h_stored, 16)

            def gather(slot, use):
                pool.wait_ge(idx_landed[slot], 16 * use)
                pool.sem_inc(gathers_start, 1)
                for t in range(TG):
                    nc.gpsimd.indirect_dma_start(
                        h_src[:, slot, t, :], None, h_table,
                        bass.IndirectOffsetOnAxis(ap=idx_sb[:, slot, t:t + 1], axis=0)).then_inc(sources_landed[slot], 16)

            def prepare(g, slot, use, first_step, last):
                if not last:
                    if not first_step:
                        pool.wait_ge(hv_sh1_ready, g)
                        pool.wait_ge(scalars_copied, g)
                    gather((slot + 1) % 4, use + (slot == 3))
                pool.wait_ge(sources_landed[slot], 16 * TG * use)
                pool.wait_ge(sh_landed[slot], 16 * use)
                if not first_step:
                    pool.wait_ge(products_ready, 2 * g - 1)
                    pool.wait_ge(dots_ready, g)
                hv = h_src[:, slot, :, MUL:F].rearrange("p t (u i) -> p t u i", i=3)
                nc.gpsimd.tensor_tensor(hv_sh1[:, :, :, :], hv, sh_sb[:, slot, :, 1:4].unsqueeze(2).to_broadcast((P, TG, MUL, 3)),
                                        ALU.mult).then_inc(hv_sh1_ready, 1)
                nc.gpsimd.tensor_tensor(lhs[:, slot % 2, :, 2 * MUL:], h_src[:, slot, :, :],
                                        sh_sb[:, slot, :, 0:1].to_broadcast((P, TG, F)), ALU.mult).then_inc(scaled_ready, 1)

            gather(0, 1)
            every_group(pool, prepare)
            with pool.If(general(pool)):
                pool.wait_ge(rows_cleared, 3)
                nc.gpsimd.iota(iota_all, pattern=[[1, ACOLS]], base=0, channel_multiplier=0,
                               allow_small_or_imprecise_dtypes=True).then_inc(iota_all_ready, 1)
                pool.wait_ge(h_stored, 32)
                pool.wait_ge(tile_summed, TILES)

                def regather(g, slot, use, first_step, last):
                    if not first_step:
                        pool.wait_ge(tile_summed, TILES + TG * g - 3 * TG)
                    nc.gpsimd.tensor_copy(idx_sb[:, slot, :], src_all[:, bass.ds(g * TG, TG)]).then_inc(idx_copied, 1)
                    pool.wait_ge(idx_copied, g + 1)
                    pool.sem_inc(gathers_start, 1)
                    for t in range(TG):
                        nc.gpsimd.indirect_dma_start(
                            rows[:, slot, t, 0:F], None, h_table,
                            bass.IndirectOffsetOnAxis(ap=idx_sb[:, slot, t:t + 1], axis=0)).then_inc(sources_again_landed[slot], 16)
                fetch_groups(pool, regather)

        @block.tensor
        def _(pe):
            def layer1(g, slot, use, first_of_all=False):
                pe.wait_ge(rad_landed[slot], 16 * use)
                if not first_of_all:
                    pe.wait_ge(silu2_ready, 2 * g)
                nc.tensor.matmul(mlp_ps, w1_sb, rad_sb[:, slot, :], start=True, stop=True).then_inc(layer1_ready, 1)

            def layer2(g, slot):
                pe.wait_ge(silu1_ready, g + 1)
                nc.tensor.matmul(mlp_ps, w2_sb[:, :], y2[:, slot % 2, :], start=True, stop=True).then_inc(layer2_ready, 1)

            pe.wait_ge(mlp_landed, 16 * 3)
            layer1(0, 0, 1, first_of_all=True)
            layer2(0, 0)
            pe.wait_ge(weights_landed, 16 * 6)
            pe.wait_ge(preamble_step, H_STEP)
            pe.wait_ge(silu2_ready, 2)
            for b in range(BLOCKS):
                m = nc.tensor.transpose(ps[0:F, b // 4, (b % 4) * P:(b % 4 + 1) * P], h_in[:, b, :], ident_sb)
                if b % 4 == 3 or b == BLOCKS - 1:
                    m.then_inc(h_turned, 1)
            pe.wait_ge(preamble_step, H_STEP + 1)
            pe.wait_ge(x_turned_ready, 2)
            for c in range(BANKS):
                pe.wait_ge(h_t_copied, c + 1)
                n = min(4, BLOCKS - 4 * c)
                nc.tensor.matmul(ps[0:F, c, 0:n * P], wself_sb[:, :], agg_t[:, c * 512:c * 512 + n * P], start=True, stop=False)
                for k in range(n):
                    m = nc.tensor.matmul(ps[0:F, c, k * P:(k + 1) * P], x_turned[:, 4 * c + k, :], ident_sb,
                                         start=False, stop=(k == n - 1))
                m.then_inc(self_ready, 1)
                if c == 4:
                    pe.wait_ge(checks_ready, 1)
                    nc.tensor.matmul(ps[0:1, 7, 0:1], checks[:, 5:6], checks[:, 6:7], start=True, stop=True
                                     ).then_inc(verdict_ready, 1)
            pe.wait_ge(self_copied, BANKS)
            pe.wait_ge(b3_rows_landed, 16 * 6)

            def weights(g, slot, half, first_step):
                if not first_step:
                    pe.wait_ge(products_ready, 2 * g + half - 1)
                q = slice(64 * half, 64 * half + 64)
                for two in range(2):
                    nc.tensor.matmul(tpw_ps[:, half, two * 512:two * 512 + 512], ones_bf[q, :],
                                     b3_rows[q, :].unsqueeze(1).to_broadcast((64, 2, NTP)), start=True, stop=False)
                for two in range(2):
                    pe.wait_ge(silu2_ready, 2 * g + two + 1)
                    for t in (2 * two, 2 * two + 1):
                        m = nc.tensor.matmul(tpw_ps[:, half, t * NTP:(t + 1) * NTP], y2[q, slot % 2, t * P:(t + 1) * P],
                                             w3_sb[q, :], start=False, stop=(t == 2 * two + 1))
                m.then_inc(weights_ready, 1)

            def count_pairs(g, half, first_step):
                pairs = (2 * half, 2 * half + 1)
                pe.wait_ge(lanes_ready, 2 * g + half + 1)
                pe.wait_ge(keys_ready, 2 * g + half + 1)
                for pair in pairs:
                    if not (first_step and pair < 2):
                        pe.wait_ge(counts_staged, 4 * g + pair - 1)
                    for t in (2 * pair, 2 * pair + 1):
                        m = nc.tensor.matmul(cnt_ps[:, pair % 2, (t % 2) * KEYS:(t % 2 + 1) * KEYS],
                                             oh_a[:, half, t % TH, :], oh_k[:, half, t % TH, :], start=True, stop=True)
                    m.then_inc(counts_ready, 1)

            def aggregate(g, half):
                pe.wait_ge(terms_ready, 2 * g + half + 1)
                pe.wait_ge(places_ready, 2 * g + half + 1)
                if half == 0:
                    pe.wait_ge(aggregate_added, g + 1)
                for t in range(half * TH, half * TH + TH):
                    m = nc.tensor.matmul(agg_ps, oh_w[:, t, :], terms[:, t, :], start=(t == 0), stop=(t == TG - 1))
                m.then_inc(half_aggregated, 1)

            def turn(g):
                pe.wait_ge(aggregate_reduced, g + 1)
                pe.sem_inc(turn_starts, 1)
                nc.tensor.matmul(turn_ps, agg_sb[:, :], ident_w[:, :], start=True, stop=True).then_inc(aggregate_turned, 1)

            def only_weights(g, slot, use, first_step, last):
                weights(g, slot, 0, first_step)
                if not last:
                    layer1(g + 1, (slot + 1) % 4, use + (slot == 3))
                weights(g, slot, 1, first_step)
                if not last:
                    layer2(g + 1, (slot + 1) % 4)

            def scatter(landed, done):
                def sum_rows(g, slot, use, first_step, last):
                    pe.wait_ge(landed[slot], use * (16 if landed is rows_landed else 16 * TG))
                    for t in range(TG):
                        pe.wait_ge(hot_tile_ready, done + TG * g + t + 1)
                        for b in range(BANKS):
                            m = nc.tensor.matmul(ps[0:F + 1, b, 0:BANK], rows[:, slot, t, :],
                                                 oh_all[:, t % 2, b * BANK:(b + 1) * BANK],
                                                 start=(first_step and t == 0), stop=(last and t == TG - 1))
                        m.then_inc(tile_summed, 1)
                every_group(pe, sum_rows)
                pe.wait_ge(tile_summed, done + TILES)
                pe.sem_inc(all_summed, 1)

            def step(g, slot, use, first_step, last):
                weights(g, slot, 0, first_step)
                if not first_step:
                    aggregate(g - 1, 0)
                if not last:
                    layer1(g + 1, (slot + 1) % 4, use + (slot == 3))
                count_pairs(g, 0, first_step)
                weights(g, slot, 1, first_step)
                if not first_step:
                    aggregate(g - 1, 1)
                if not last:
                    layer2(g + 1, (slot + 1) % 4)
                if not first_step:
                    turn(g - 1)
                count_pairs(g, 1, first_step)

            with pe.If(dense(pe)):
                every_group(pe, step)
                aggregate(GROUPS - 1, 0)
                aggregate(GROUPS - 1, 1)
                turn(GROUPS - 1)
            with pe.Else():
                every_group(pe, only_weights)
                pe.wait_ge(products_ready, 2 * GROUPS)
                scatter(rows_landed, 0)

            pe.wait_ge(layer0_done, 1)
            for half, (b0, b1) in enumerate(HALVES):
                for b in range(b0, b1):
                    m = nc.tensor.transpose(ps[:, half, (b - b0) * F:(b - b0 + 1) * F], agg_t[:, b * P:(b + 1) * P],
                                            ident_w[0:F, 0:F])
                m.then_inc(x1_ready, 1)
            with pe.If(dense(pe)):
                for part, (k0, k1) in enumerate(HALVES):
                    pe.wait_ge(parts_ready, part + 1)
                    if part == 0:
                        pe.wait_ge(x1_copied, 2)
                    for b in (*range(BLOCKS - 2), BLOCKS - 1, BLOCKS - 2):
                        cols = min(P, ACOLS - b * P)
                        closes = part == 1 and (b % BB == BB - 1 or b == BLOCKS - 2)
                        for k in range(k0, k1):
                            m = nc.tensor.matmul(result_ps(b)[0:cols], counts[:, k, b * P:b * P + cols],
                                                 parts[:, k, :], start=(b % BB == 0 and k == 0),
                                                 stop=(closes and k == BLOCKS - 1))
                        if closes:
                            m.then_inc(sums_ready, 1)
            with pe.Else():
                pe.wait_ge(x1_copied, 2)
                pe.wait_ge(parts_ready, 2)
                scatter(sources_again_landed, TILES)
                pe.wait_ge(sums_copied, 1)
                pe.wait_ge(spread_landed, 16)
                for b in range(BLOCKS):
                    cols = min(P, ACOLS - b * P)
                    m = nc.tensor.matmul(result_ps(b)[0:cols], sums_t[:, b * P:b * P + cols], spread_sb, start=True, stop=True)
                    if b % BB == BB - 1 or b == BLOCKS - 1:
                        m.then_inc(sums_ready, 1)

        @block.scalar
        def _(act):
            def root(variance_ready, count):
                act.wait_ge(variance_ready, count)
                nc.scalar.activation(stat[:, 1, :], stat[:, 3, :], ACT.Sqrt).then_inc(root_ready, 1)

            def clear(first_row, end):
                n = (end - first_row) * ACOLS // 2
                return nc.scalar.copy(cleared(first_row, end), zero[:, :].to_broadcast((P, n)))

            def silu1(g, slot, first_step):
                act.wait_ge(layer1_ready, g + 1)
                if not first_step:
                    act.wait_ge(weights_ready, 2 * g - 2)
                nc.scalar.activation(y2[:, slot % 2, :], mlp_ps, ACT.Silu, bias=b12_sb[:, 0:1]).then_inc(silu1_ready, 1)

            def silu2(g, slot):
                act.wait_ge(layer2_ready, g + 1)
                for two in (slice(0, 256), slice(256, 512)):
                    nc.scalar.activation(y2[:, slot % 2, two], mlp_ps[:, two], ACT.Silu, bias=b12_sb[:, 1:2]
                                         ).then_inc(silu2_ready, 1)

            act.wait_ge(zero_ready, 1)
            clear(POOL_ROWS, POOL_ROWS + ACT_ROWS).then_inc(rows_cleared, 1)
            act.wait_ge(x_landed, 32)
            nc.scalar.copy(x_turned[:, :, 0:MUL], x_in[:, :, 0:MUL]).then_inc(x_turned_ready, 1)
            nc.scalar.copy(x_turned[:, :, MUL:F].rearrange("p b (i w) -> p b i w", i=3),
                           x_in[:, :, MUL:F].rearrange("p b (w i) -> p b i w", i=3)).then_inc(x_turned_ready, 1)
            root(preamble_step, VARIANCE_STEP)
            act.wait_ge(mlp_landed, 16 * 3)
            silu1(0, 0, True)
            silu2(0, 0)
            act.wait_ge(weights_landed, 16 * 6)
            for b in range(BANKS):
                act.wait_ge(h_turned, b + 1)
                n = min(4, BLOCKS - 4 * b) * P
                nc.scalar.copy(agg_t[:, b * 512:b * 512 + n], ps[0:F, b, 0:n]).then_inc(h_t_copied, 1)
            for c in range(BANKS):
                act.wait_ge(self_ready, c + 1)
                n = min(4, BLOCKS - 4 * c) * P
                nc.scalar.copy(agg_t[:, c * 512:c * 512 + n], ps[0:F, c, 0:n]).then_inc(self_copied, 1)

            def lanes(g, slot, half, first_step):
                act.wait_ge(current_ready, g + 1)
                if not first_step:
                    act.wait_ge(counts_ready, 4 * g + 2 * half - 2)
                for k in range(TH):
                    m = nc.scalar.activation(oh_a[:, half, k, :], iota_a[:, :], ACT.Abs, scale=-1.0,
                                             bias=cur[:, slot % 4, 0, half * TH + k:half * TH + k + 1])
                m.then_inc(lane_distances_ready, 1)
                act.wait_ge(lane_distances_ready, 2 * g + half + 1)
                nc.scalar.activation(oh_a[:, half, :, :], oh_a[:, half, :, :], ACT.Relu, scale=-1.0, bias=1.0
                                     ).then_inc(lanes_ready, 1)

            def places(g, slot, half, first_step):
                act.wait_ge(current_ready, g + 1)
                if not first_step:
                    act.wait_ge(half_aggregated, 2 * g + half - 1)
                ts = slice(half * TH, half * TH + TH)
                for t in range(ts.start, ts.stop):
                    m = nc.scalar.activation(oh_w[:, t, :], iota_w[:, :], ACT.Abs, scale=-1.0,
                                             bias=cur[:, slot % 4, 2, t:t + 1])
                m.then_inc(place_distances_ready, 1)
                act.wait_ge(place_distances_ready, 2 * g + half + 1)
                nc.scalar.activation(oh_w[:, ts, :], oh_w[:, ts, :], ACT.Relu, scale=-1.0, bias=1.0).then_inc(places_ready, 1)

            def copy_scalars(g, slot, use, first_step):
                act.wait_ge(sources_landed[slot], 16 * TG * use)
                if not first_step:
                    act.wait_ge(products_ready, 2 * g - 1)
                nc.scalar.copy(lhs[:, slot % 2, :, 0:MUL], h_src[:, slot, :, 0:MUL]).then_inc(scalars_copied, 1)

            def unload(g, half, first_step):
                for pair in (2 * half, 2 * half + 1):
                    act.wait_ge(counts_ready, 4 * g + pair + 1)
                    if not (first_step and pair < 2):
                        act.wait_ge(counts_added, TG * g + 2 * pair - 2)
                    nc.scalar.copy(stage[:, pair % 2, :, :].rearrange("p a b -> p (a b)"), cnt_ps[:, pair % 2, :]
                                   ).then_inc(counts_staged, 1)

            def step(g, slot, use, first_step, last):
                if not last:
                    silu1(g + 1, (slot + 1) % 4, first_step)
                unload(g, 0, first_step)
                lanes(g, slot, 1, first_step)
                if not last:
                    silu2(g + 1, (slot + 1) % 4)
                places(g, slot, 0, first_step)
                if not last:
                    copy_scalars(g + 1, (slot + 1) % 4, use + (slot == 3), first_step)
                    lanes(g + 1, slot + 1, 0, False)
                unload(g, 1, first_step)
                places(g, slot, 1, first_step)

            copy_scalars(0, 0, 1, True)

            def only_silu(g, slot, use, first_step, last):
                if not last:
                    copy_scalars(g + 1, (slot + 1) % 4, use + (slot == 3), first_step)
                    silu1(g + 1, (slot + 1) % 4, first_step)
                    silu2(g + 1, (slot + 1) % 4)
                act.wait_ge(messages_ready, g + 1)
                act.dma_start(msg_table[bass.ds(g, 1), :, :].rearrange("a p n -> (a p) n"),
                              msg[:, :, :].rearrange("p t f -> p (t f)")).then_inc(messages_stored, 16)

            with act.If(dense(act)):
                lanes(0, 0, 0, True)
                every_group(act, step)
            with act.Else():
                every_group(act, only_silu)
                act.wait_ge(messages_stored, 16 * GROUPS)
            for k, (b0, b1) in enumerate(HALVES):
                act.wait_ge(x1_ready, k + 1)
                turned = nodes(ps[:, k, 0:(b1 - b0) * F])
                nc.scalar.copy(x_1[:, b0:b1, 0:MUL], turned[:, :, 0:MUL])
                nc.scalar.copy(x_1[:, b0:b1, MUL:F].rearrange("p b (w i) -> p b i w", i=3),
                               turned[:, :, MUL:F].rearrange("p b (i w) -> p b i w", i=3)).then_inc(x1_copied, 1)
            for k, (b0, b1) in enumerate(HALVES):
                act.wait_ge(second_step, k * HALF_STEPS + VARIANCE_STEP - 1)
                nc.scalar.activation(stat[:, 1, b0:b1], stat[:, 3, b0:b1], ACT.Sqrt).then_inc(root_ready, 1)

        @block.vector
        def _(dve):
            n_init = [0]

            def link(ins):
                n_init[0] += 1
                ins.then_inc(preamble_step, 1)
                dve.wait_ge(preamble_step, n_init[0])

            def layer_norm(of, to, xc, sq, step, root, b0, b1):
                def st(k):
                    return stat[:, k, b0:b1]

                def wide(k):
                    return st(k).unsqueeze(2).to_broadcast((P, b1 - b0, F))
                of, to, xc, sq = (a[:, b0:b1, :] for a in (of, to, xc, sq))
                step(nc.vector.tensor_reduce(st(0), of, X, ALU.add))
                step(nc.vector.tensor_scalar(st(1), st(0), 1.0 / F, None, ALU.mult))
                step(nc.vector.tensor_tensor(xc, of, wide(1), ALU.subtract))
                step(nc.vector.tensor_tensor(sq, xc, xc, ALU.mult))
                step(nc.vector.tensor_reduce(st(2), sq, X, ALU.add))
                step(nc.vector.tensor_scalar(st(3), st(2), 1.0 / F, EPS, ALU.mult, ALU.add))
                dve.wait_ge(root_ready, root)
                step(nc.vector.reciprocal(st(0), st(1)))
                step(nc.vector.tensor_tensor(st(2), st(0), st(0), ALU.mult))
                step(nc.vector.tensor_tensor(st(2), st(2), st(3), ALU.mult))
                step(nc.vector.tensor_scalar(st(2), st(2), -0.5, 1.5, ALU.mult, ALU.add))
                step(nc.vector.tensor_tensor(st(0), st(0), st(2), ALU.mult))
                step(nc.vector.scalar_tensor_tensor(out=to, in0=xc, scalar=0.0, in1=wide(0), op0=ALU.max, op1=ALU.mult))

            link(nc.vector.memset(x_in[:, BLOCKS - 1:BLOCKS, :], 0.0))
            nc.vector.memset(zero[:, :], 0.0).then_inc(zero_ready, 1)
            dve.wait_ge(zero_ready, 1)
            nc.vector.memset(ones_bf[:, :], 1.0)
            nc.vector.memset(b3_rows[:, :], 0.0).then_inc(b3_step, 1)
            dve.wait_ge(x_landed, 32)
            layer_norm(x_in, h_in, xc_in, sq_in, link, 1, 0, BLOCKS)
            dve.wait_ge(weights_landed, 16 * 6)
            nc.vector.tensor_scalar(wself_sb[:, :], wself_sb[:, :], C_SELF, None, ALU.mult)
            for start, end, by in ((0, 64, C_MSG), (64, 128, C_VEC), (128, NTP, C_MSG)):
                nc.vector.tensor_scalar(w3_sb[:, start:end], w3_sb[:, start:end], by, None, ALU.mult)
                scaled = nc.vector.tensor_scalar(b3_f[:, 1, start:end], b3_f[:, 0, start:end], by, None, ALU.mult)
            link(scaled)
            nc.vector.tensor_copy(b3_parts[:, 0, :], b3_f[:, 1, :]).then_inc(b3_step, 1)
            dve.wait_ge(b3_step, 2)
            link(nc.vector.tensor_tensor(b3_f[:, 0, :], b3_f[:, 1, :], b3_parts[:, 0, :], ALU.subtract))
            nc.vector.tensor_copy(b3_parts[:, 1, :], b3_f[:, 0, :]).then_inc(b3_step, 1)
            dve.wait_ge(b3_step, 3)
            nc.vector.tensor_tensor(b3_parts[:, 2, :], b3_f[:, 0, :], b3_parts[:, 1, :], ALU.subtract).then_inc(b3_step, 1)

            dve.wait_ge(edges_landed, 48)
            link(nc.vector.tensor_scalar(scratch_i, src_all[:, :], P - 1, None, ALU.bitwise_and))
            link(nc.vector.tensor_copy(tables[:, 0, :], scratch_i))
            link(nc.vector.tensor_tensor(scratch_f, dst_all, first_bc, ALU.subtract))
            nc.vector.tensor_reduce(checks[:, 0:1], scratch_f, X, ALU.max)
            nc.vector.tensor_reduce(checks[:, 1:2], scratch_f, X, ALU.min)
            link(nc.vector.tensor_scalar(scratch_i, src_all[:, :], 7, 3, ALU.logical_shift_right, ALU.logical_shift_left))
            link(nc.vector.tensor_tensor(tables[:, 1, :], scratch_f, scratch_i, ALU.add))

            def grouped(flat):
                return flat.rearrange("p (g t) -> p g t", t=TG)
            link(nc.vector.tensor_tensor(grouped(tables[:, 2, :]), grouped(dst_all),
                                         grouped(first_bc)[:, :, 0:1].to_broadcast((P, GROUPS, TG)), ALU.subtract))
            nc.vector.tensor_reduce(checks[:, 2:3], tables[:, 2:3, :], X, ALU.max)
            nc.vector.tensor_reduce(checks[:, 3:4], tables[:, 2:3, :], X, ALU.min)
            link(nc.vector.tensor_tensor(scratch_f[:, 0:TILES - SPAN + 1], first_bc[:, SPAN - 1:TILES],
                                         first_bc[:, 0:TILES - SPAN + 1], ALU.subtract))
            link(nc.vector.tensor_reduce(checks[:, 4:5], scratch_f[:, 0:TILES - SPAN + 1], X, ALU.min))
            for k, (op, bound) in enumerate(((ALU.is_le, WT - 1), (ALU.is_ge, 0), (ALU.is_le, WG - 1), (ALU.is_ge, 0),
                                             (ALU.is_ge, 1))):
                nc.vector.tensor_scalar(checks[:, k:k + 1], checks[:, k:k + 1], float(bound), None, op)
            link(nc.vector.memset(checks[:, 6:7], 1.0))
            nc.vector.tensor_reduce(checks[:, 5:6], checks[:, 0:5], X, ALU.min).then_inc(checks_ready, 1)
            n = (EARLY - POOL_ROWS - ACT_ROWS) * ACOLS // 2
            nc.vector.tensor_copy(cleared(POOL_ROWS + ACT_ROWS, EARLY), zero[:, :].to_broadcast((P, n))).then_inc(rows_cleared, 1)
            dve.wait_ge(verdict_ready, 1)
            nc.vector.tensor_scalar(dense_sb[:, :], ps[0:1, 7, 0:1], P - 0.5, None, ALU.is_ge).then_inc(dense_ready, 1)
            dve.wait_ge(h_stored, 16)
            dve.wait_ge(b3_rows_landed, 16 * 6)
            dve.wait_ge(b3_step, 4)
            dve.wait_ge(iotas_ready, 3)

            def current(g, slot):
                nc.vector.tensor_copy(cur[:, slot % 4, :, :], tables[:, :, bass.ds(g * TG, TG)]).then_inc(current_ready, 1)

            def keys(g, slot, half, first_step):
                dve.wait_ge(current_ready, g + 1)
                if not first_step:
                    dve.wait_ge(counts_ready, 4 * g + 2 * half - 2)
                for k in range(TH):
                    t = half * TH + k
                    m = nc.vector.tensor_scalar(oh_k[:, half, k, :], iota_k[:, :], cur[:, slot % 4, 1, t:t + 1], None,
                                                ALU.is_equal)
                m.then_inc(keys_ready, 1)

            def dots(g, slot, first_step):
                dve.wait_ge(hv_sh1_ready, g + 1)
                if not first_step:
                    dve.wait_ge(products_ready, 2 * g - 2)
                nc.vector.tensor_reduce(lhs[:, slot % 2, :, MUL:2 * MUL], hv_sh1[:, :, :, :], X, ALU.add
                                        ).then_inc(dots_ready, 1)

            def products(g, slot, half, first_step, between, messages_used=True):
                ts = slice(half * TH, half * TH + TH)
                w = tpw_ps[:, half, :].rearrange("p (t n) -> p t n", n=NTP)
                if half == 0:
                    dve.wait_ge(dots_ready, g + 1)
                    dve.wait_ge(scaled_ready, g + 1)
                    dve.wait_ge(scalars_copied, g + 1)
                dve.wait_ge(weights_ready, 2 * g + half + 1)
                if not (first_step and half == 0):
                    dve.wait_ge(scalars_summed, 2 * g + half)
                nc.vector.tensor_tensor(prod_s.rearrange("p t (u w) -> p t u w", w=MUL),
                                        w[:, :, 0:192].rearrange("p t (u w) -> p t u w", w=MUL),
                                        lhs[:, slot % 2, ts, 0:3 * MUL].unsqueeze(3).to_broadcast((P, TH, 24, MUL)), ALU.mult)
                between(0)
                if messages_used and not first_step:
                    dve.wait_ge(half_aggregated, 2 * g + half - 1)
                for i in range(3):
                    m = nc.vector.tensor_tensor(vec_terms[:, ts, i, 0:64].rearrange("p t (u w) -> p t u w", w=MUL),
                                                w[:, :, 192:256].rearrange("p t (u w) -> p t u w", w=MUL),
                                                lhs_v[:, slot % 2, ts, i, :].unsqueeze(3).to_broadcast((P, TH, MUL, MUL)),
                                                ALU.mult)
                    if i < 2:
                        between(i + 1)
                m.then_inc(products_ready, 1)
                between(3)

            def scalar_sums(g, half):
                ts = slice(half * TH, half * TH + TH)
                dve.wait_ge(products_ready, 2 * g + half + 1)
                nc.vector.tensor_reduce(t01[:, :, :], prod_s[:, :, 0:64].rearrange("p t (u w) -> p t w u", w=MUL), X, ALU.add
                                        ).then_inc(t01_ready, 1)
                nc.vector.tensor_reduce(terms[:, ts, VEC:MV], prod_s[:, :, 64:192].rearrange("p t (u w) -> p t w u", w=MUL), X,
                                        ALU.add).then_inc(scalars_summed, 1)

            def vector_part(g, slot, half):
                ts = slice(half * TH, half * TH + TH)
                dve.wait_ge(t01_ready, 2 * g + half + 1)
                nc.vector.tensor_tensor(vec_terms[:, ts, :, 64:72], t01[:, :, :].unsqueeze(2).to_broadcast((P, TH, 3, MUL)),
                                        sh_sb[:, slot, ts, 1:4].unsqueeze(3).to_broadcast((P, TH, 3, MUL)), ALU.mult
                                        ).then_inc(terms_ready, 1)

            def add_count(g, t, base):
                dve.wait_ge(counts_staged, 4 * g + t // 2 + 1)
                dve.wait_ge(counts_added, TG * g + t)
                to = counts[:, :, bass.ds(base, WT)]
                nc.vector.tensor_tensor(to, to, stage[:, t // 2 % 2, t % 2, :].rearrange("p (b w) -> p b w", w=WT), ALU.add
                                        ).then_inc(counts_added, 1)

            def reduce_aggregate(g):
                dve.wait_ge(half_aggregated, 2 * g + 2)
                nc.vector.tensor_copy(agg_sb[:, 0:MUL], agg_ps[:, VEC:MV])
                nc.vector.tensor_reduce(agg_sb[:, MUL:F].rearrange("p (i w) -> p i w", i=3),
                                        agg_ps[:, 0:VEC].rearrange("p (i u w) -> p i w u", i=3, u=US), X, ALU.add
                                        ).then_inc(aggregate_reduced, 1)

            def add_aggregate(g, base):
                dve.wait_ge(aggregate_turned, g + 1)
                dve.wait_ge(aggregate_added, g + 1)
                to = agg_t[:, bass.ds(base, WG)]
                nc.vector.tensor_tensor(to, to, turn_ps, ALU.add).then_inc(aggregate_added, 1)

            def bases_of(tile, n):
                return nc.values_load_multi_w_load_instructions(
                    first_sb[0:1, bass.ds(tile, n)], engines=[mybir.EngineType.DVE], min_val=0, max_val=N,
                    skip_runtime_bounds_check_because="destinations are node numbers, and the padding's is N")[1]

            def nothing(k):
                pass

            def step(g, slot, use, first_step, last):
                if first_step:
                    late, now, before = nothing, bases_of(0, TH), None
                else:
                    bases = bases_of(TG * g - TG, TG + TH)
                    late, now, before = bases[TH:TG], bases[TG:], bases[0]
                if not last:
                    if not first_step:
                        dve.wait_ge(lanes_ready, 2 * g - 1)
                        dve.wait_ge(places_ready, 2 * g - 1)
                    current(g + 1, slot + 1)
                keys(g, slot, 1, first_step)
                products(g, slot, 0, first_step, nothing if first_step else lambda k: add_count(g - 1, TH + k, late[k]))
                scalar_sums(g, 0)
                vector_part(g, slot, 0)

                if first_step:
                    dve.wait_ge(self_ready, BANKS)
                    nc.vector.tensor_copy(early[:, INPUTS:], zero[:, :].to_broadcast((P, EARLY_WORDS - INPUTS))
                                          ).then_inc(rows_cleared, 1)
                    dve.wait_ge(rows_cleared, 4)

                def others(k):
                    add_count(g, k, now[k])
                    if k == 0 and not first_step:
                        reduce_aggregate(g - 1)
                products(g, slot, 1, first_step, others)
                if not last:
                    keys(g + 1, slot + 1, 0, False)
                    dots(g + 1, slot + 1, first_step)
                if not first_step:
                    add_aggregate(g - 1, before)
                scalar_sums(g, 1)
                vector_part(g, slot, 1)

            def only_messages(g, slot, use, first_step, last):
                if not first_step:
                    dve.wait_ge(messages_ready, g)
                for half in range(2):
                    if half == 1 and not last:
                        dots(g + 1, slot + 1, first_step)
                    products(g, slot, half, first_step, nothing, False)
                    scalar_sums(g, half)
                    vector_part(g, slot, half)
                dve.wait_ge(terms_ready, 2 * g + 2)
                dve.wait_ge(scalars_summed, 2 * g + 2)
                if not first_step:
                    dve.wait_ge(messages_stored, 16 * g)
                nc.vector.tensor_copy(msg[:, :, 0:MUL], terms[:, :, VEC:MV])
                for i in range(3):
                    m = nc.vector.tensor_reduce(msg[:, :, MUL + i * MUL:2 * MUL + i * MUL],
                                                vec_terms[:, :, i, :].rearrange("p t (u w) -> p t w u", u=US), X, ALU.add)
                m.then_inc(messages_ready, 1)

            def all_places(done):
                def tiles(g, slot, use, first_step, last):
                    dve.wait_ge(hot_tile_ready, done + TG * g)
                    nc.vector.tensor_copy(cur[:, 0, 0, :], dst_all[:, bass.ds(g * TG, TG)]).then_inc(current_ready, 1)
                    dve.wait_ge(current_ready, done // TG + g + 1)
                    for t in range(TG):
                        if not (first_step and t < 2):
                            dve.wait_ge(tile_summed, done + TG * g + t - 1)
                        nc.vector.tensor_scalar(oh_all[:, t % 2, :], iota_all, cur[:, 0, 0, t:t + 1], None, ALU.is_equal
                                                ).then_inc(hot_tile_ready, 1)
                every_group(dve, tiles)

            with dve.If(dense(dve)):
                dve.wait_ge(dense_ready, 1)
                dve.wait_ge(x_turned_ready, 2)
                dve.wait_ge(h_turned, BANKS)
                nc.vector.tensor_copy(early[:, 0:INPUTS], zero[:, :].to_broadcast((P, INPUTS)))
                dve.sem_inc(aggregate_added, 1)
                current(0, 0)
                keys(0, 0, 0, True)
                dots(0, 0, True)
                every_group(dve, step)
                bases = bases_of(TILES - TG, TG)
                for t in range(TH, TG):
                    add_count(GROUPS - 1, t, bases[t])
                reduce_aggregate(GROUPS - 1)
                add_aggregate(GROUPS - 1, bases[0])
                dve.wait_ge(aggregate_added, GROUPS + 1)
            with dve.Else():
                dve.wait_ge(rows_cleared, 3)
                dots(0, 0, True)
                every_group(dve, only_messages)
                dve.wait_ge(scaled_ready, GROUPS)
                nc.vector.memset(rows[:, :, :, F:F + 1], 1.0).then_inc(ones_ready, 1)
                dve.wait_ge(iota_all_ready, 1)
                all_places(0)
                dve.wait_ge(all_summed, 1)
                for b in range(BANKS):
                    m = nc.vector.tensor_tensor(agg_t[:, b * BANK:(b + 1) * BANK], agg_t[:, b * BANK:(b + 1) * BANK],
                                                ps[0:F, b, 0:BANK], ALU.add)
                m.then_inc(aggregate_added, 1)
                dve.wait_ge(aggregate_added, 1)
            dve.sem_inc(layer0_done, 1)

            n_second = [0]

            def then(ins):
                n_second[0] += 1
                ins.then_inc(second_step, 1)
                dve.wait_ge(second_step, n_second[0])
            nc.vector.memset(parts[:, :, 2 * F:PARTS], 1.0)
            for k, (b0, b1) in enumerate(HALVES):
                dve.wait_ge(x1_copied, k + 1)
                layer_norm(x_1, h_1, xc_1, sq_1, then, k + 2, b0, b1)
                dve.sem_inc(h1_ready, 1)
                then(nc.vector.tensor_copy(parts[:, b0:b1, 0:F], h_1[:, b0:b1, :]))
                then(nc.vector.tensor_tensor(xc_1[:, b0:b1, :], h_1[:, b0:b1, :], parts[:, b0:b1, 0:F], ALU.subtract))
                nc.vector.tensor_scalar(parts[:, b0:b1, F:2 * F], xc_1[:, b0:b1, :], LOW, None, ALU.mult).then_inc(parts_ready, 1)
            with dve.If(general(dve)):
                all_places(TILES)
                dve.wait_ge(all_summed, 2)
                dve.wait_ge(parts_ready, 2)
                for b in range(BANKS):
                    m = nc.vector.tensor_copy(sums_t[:, b * BANK:(b + 1) * BANK], ps[0:F + 1, b, 0:BANK])
                m.then_inc(sums_copied, 1)
            for bank, b0 in enumerate(range(0, BLOCKS, BB)):
                b1 = min(b0 + BB, BLOCKS)
                dve.wait_ge(sums_ready, bank + 1)
                v = ps[:, bank, 0:(b1 - b0) * PARTS].rearrange("p (b f) -> p b f", f=PARTS)
                degree, inverse = stat[:, 0, b0:b1], stat[:, 1, b0:b1]
                nc.vector.tensor_scalar(xc_1[:, b0:b1, :], v[:, :, F:2 * F], 1.0 / LOW, None, ALU.mult)
                then(nc.vector.tensor_scalar(degree.unsqueeze(2), v[:, :, 2 * F:PARTS], 1.0, None, ALU.max))
                nc.vector.reciprocal(inverse, degree)
                then(nc.vector.tensor_tensor(h_1[:, b0:b1, :], xc_1[:, b0:b1, :], v[:, :, 0:F], ALU.add))
                then(nc.vector.tensor_tensor(h_1[:, b0:b1, :], h_1[:, b0:b1, :],
                                             inverse.unsqueeze(2).to_broadcast((P, b1 - b0, F)), ALU.mult))
                nc.vector.tensor_tensor(h_1[:, b0:b1, :], h_1[:, b0:b1, :], x_1[:, b0:b1, :], ALU.add).then_inc(result_ready, 1)


def kernel(x, src, dst, edge_attr_4, edge_attr_8, L0_gnn_W1, L0_gnn_b1, L0_gnn_W2, L0_gnn_b2, L0_gnn_W3, L0_gnn_b3,
           L0_gnn_Ws, L0_gnn_Wv):
    import numpy as np
    import concourse.bacc as bacc
    from concourse.bass_utils import run_bass_kernel_spmd

    f32, i32 = np.float32, np.int32
    padded = TILES * P

    def pad(a, fill=0):
        a = np.asarray(a)
        to = np.full((padded,) + a.shape[1:], fill, a.dtype)
        to[:E] = a
        return to

    src_p = np.ascontiguousarray(pad(src).reshape(TILES, P).T)
    dst_p = np.ascontiguousarray(pad(dst, N).reshape(TILES, P).T)
    sh_p = np.ascontiguousarray(pad(edge_attr_4).reshape(GROUPS, TG, P, 4).transpose(0, 2, 1, 3).reshape(GROUPS, P, TG * 4))
    rad_p = np.ascontiguousarray(pad(edge_attr_8).reshape(GROUPS, 2, TH * P, NB).transpose(0, 1, 3, 2)
                                 .reshape(GROUPS, 2 * NB, TH * P))

    def in_order(a):
        return np.concatenate([a[:, 128:192], a[:, 64:128], a[:, 0:64], a[:, 192:]], axis=1)
    w1 = np.zeros((2 * NB, P), f32)
    w2 = np.zeros((P, P), f32)
    w3 = np.zeros((P, NTP), f32)
    b12 = np.zeros((P, 2), f32)
    for k in range(2):
        w1[k * NB:(k + 1) * NB, k * HR:(k + 1) * HR] = L0_gnn_W1
        w2[k * HR:(k + 1) * HR, k * HR:(k + 1) * HR] = L0_gnn_W2
        w3[k * HR:(k + 1) * HR] = in_order(np.asarray(L0_gnn_W3))
        b12[k * HR:(k + 1) * HR, 0] = L0_gnn_b1
        b12[k * HR:(k + 1) * HR, 1] = L0_gnn_b2
    wself = np.zeros((F, F), f32)
    wself[0:MUL, 0:MUL] = L0_gnn_Ws
    for i in range(3):
        wself[MUL + i:F:3, MUL + i * MUL:MUL + (i + 1) * MUL] = L0_gnn_Wv
    spread = np.zeros((F + 1, PARTS), f32)
    spread[range(F), range(F)] = 1
    spread[F, 2 * F] = 1
    arrays = {
        "x": np.asarray(x), "src": src_p, "dst": dst_p, "first": np.ascontiguousarray(dst_p[0:1, :]), "sh": sh_p, "rad": rad_p,
        "w1": w1, "w2": w2, "w3": w3, "bias12": b12, "b3": in_order(np.asarray(L0_gnn_b3).reshape(1, NTP)), "wself": wself,
        "ident": np.eye(P, dtype=f32), "spread": spread,
    }
    nc = bacc.Bacc("TRN2", target_bir_lowering=False, num_devices=1)
    args = [nc.dram_tensor(n, a.shape, mybir.dt.from_np(a.dtype), kind="ExternalInput").ap() for n, a in arrays.items()]
    out = nc.dram_tensor("out_0", (N, F), F32, kind="ExternalOutput").ap()
    build(nc, *args, out)
    return run_bass_kernel_spmd(nc, [arrays], core_ids=[0]).results[0]["out_0"]
```
